# Optimizing a Trainium2 kernel written in Bass

```python
import numpy as np
import jax
import jax.numpy as jnp

def _softmax(x, axis=-1):
    return jax.nn.softmax(x, axis=axis)

def _gelu(x):
    return jax.nn.gelu(x, approximate=True)

def _silu(x):
    return jax.nn.silu(x)

def _sigmoid(x):
    return jax.nn.sigmoid(x)

def _layernorm(x, axis=-1, eps=1e-05):
    m = jnp.mean(x, axis=axis, keepdims=True)
    v = jnp.var(x, axis=axis, keepdims=True)
    return (x - m) / jnp.sqrt(v + eps)

def _scatter_add(tgt, idx, src, axis=0):
    return tgt.at[idx].add(src)

def _segment_sum(src, seg, n):
    return jax.ops.segment_sum(src, seg, n)
kernel_name = 'mk_sandwich_d1_jaxref_r8_345f2d'

def setup_inputs(seed: int=0):
    np.random.seed(seed)
    _w = jnp.asarray

    def _L0_attn_setup():
        import jax, jax.numpy as jnp
        import numpy as np
        D_MODEL = 256
        STATE = 16
        KCONV = 4
        EXPAND = 2
        D_INNER = D_MODEL * EXPAND
        EPS = 1e-05

        def _silu(v):
            return v * jax.nn.sigmoid(v)
        key = jax.random.key(seed)
        ks = jax.random.split(key, 10)
        s = 0.02
        x = jax.random.normal(ks[0], (2, 256, D_MODEL), dtype=jnp.float32)
        norm_w = jnp.ones((D_MODEL,), jnp.float32)
        in_proj_w = jax.random.normal(ks[1], (D_INNER * 2, D_MODEL), jnp.float32) * s
        conv_w = jax.random.normal(ks[2], (D_INNER, 1, KCONV), jnp.float32) * s
        conv_b = jnp.zeros((D_INNER,), jnp.float32)
        x_proj_w = jax.random.normal(ks[3], (STATE * 2 + 1, D_INNER), jnp.float32) * s
        dt_w = jax.random.normal(ks[4], (D_INNER, 1), jnp.float32) * s
        dt_b = jnp.zeros((D_INNER,), jnp.float32)
        A_log = jnp.log(jnp.broadcast_to(jnp.arange(1, STATE + 1, dtype=jnp.float32)[None, :], (D_INNER, STATE)))
        D_param = jnp.ones((D_INNER,), jnp.float32)
        out_proj_w = jax.random.normal(ks[5], (D_MODEL, D_INNER), jnp.float32) * s
        return {'x': x, 'norm_w': norm_w, 'in_proj_w': in_proj_w, 'conv_w': conv_w, 'conv_b': conv_b, 'x_proj_w': x_proj_w, 'dt_w': dt_w, 'dt_b': dt_b, 'A_log': A_log, 'D_param': D_param, 'out_proj_w': out_proj_w}
    _L0_attn_in = _L0_attn_setup()

    def _L0_ffn_setup():
        import jax, jax.numpy as jnp
        import numpy as np
        E = 32
        D = 256
        I = 176
        NG = 8
        TKG = 4
        TOPK = 8
        SCALE = 2.5
        SI = I * 2

        def _route(x, router_weight, e_bias):
            T = x.shape[0]
            scores = jax.nn.sigmoid(x @ router_weight.T)
            sfc = scores + e_bias[None, :]
            grp = sfc.reshape(T, NG, E // NG)
            top2, _ = jax.lax.top_k(grp, 2)
            group_scores = top2.sum(-1)
            _, gidx = jax.lax.top_k(group_scores, TKG)
            gmask = jnp.zeros((T, NG), sfc.dtype).at[jnp.arange(T)[:, None], gidx].set(1.0)
            smask = jnp.repeat(gmask, E // NG, axis=1)
            masked = jnp.where(smask > 0, sfc, 0.0)
            _, topk_idx = jax.lax.top_k(masked, TOPK)
            topk_w = jnp.take_along_axis(scores, topk_idx, axis=1)
            topk_w = topk_w / (topk_w.sum(-1, keepdims=True) + 1e-20)
            topk_w = topk_w * SCALE
            combine = jnp.zeros((T, E), scores.dtype).at[jnp.arange(T)[:, None], topk_idx].add(topk_w)
            return combine
        key = jax.random.key(seed)
        ks = jax.random.split(key, 8)
        s = 0.02
        return {'hidden_states': jax.random.normal(ks[0], (2, 256, D), jnp.float32), 'router_weight': jax.random.normal(ks[1], (E, D), jnp.float32) * s, 'e_bias': jnp.zeros((E,), jnp.float32), 'Wg': jax.random.normal(ks[2], (E, I, D), jnp.float32) * s, 'Wu': jax.random.normal(ks[3], (E, I, D), jnp.float32) * s, 'Wd': jax.random.normal(ks[4], (E, D, I), jnp.float32) * s, 'sWg': jax.random.normal(ks[5], (SI, D), jnp.float32) * s, 'sWu': jax.random.normal(ks[6], (SI, D), jnp.float32) * s, 'sWd': jax.random.normal(ks[7], (D, SI), jnp.float32) * s}
    _L0_ffn_in = _L0_ffn_setup()
    _d = {'L0_attn_x': _L0_attn_in['x'], 'L0_attn_norm_w': _L0_attn_in['norm_w'], 'L0_attn_in_proj_w': _L0_attn_in['in_proj_w'], 'L0_attn_conv_w': _L0_attn_in['conv_w'], 'L0_attn_conv_b': _L0_attn_in['conv_b'], 'L0_attn_x_proj_w': _L0_attn_in['x_proj_w'], 'L0_attn_dt_w': _L0_attn_in['dt_w'], 'L0_attn_dt_b': _L0_attn_in['dt_b'], 'L0_attn_A_log': _L0_attn_in['A_log'], 'L0_attn_D_param': _L0_attn_in['D_param'], 'L0_attn_out_proj_w': _L0_attn_in['out_proj_w'], 'L0_ffn_router_weight': _L0_ffn_in['router_weight'], 'L0_ffn_e_bias': _L0_ffn_in['e_bias'], 'L0_ffn_Wg': _L0_ffn_in['Wg'], 'L0_ffn_Wu': _L0_ffn_in['Wu'], 'L0_ffn_Wd': _L0_ffn_in['Wd'], 'L0_ffn_sWg': _L0_ffn_in['sWg'], 'L0_ffn_sWu': _L0_ffn_in['sWu'], 'L0_ffn_sWd': _L0_ffn_in['sWd']}
    _x0 = _d['L0_attn_x']
    _d['L0_attn_x'] = jax.random.normal(jax.random.fold_in(jax.random.key(seed), 1), (4, 256, 256), dtype=_x0.dtype)
    del _x0
    return _d

def reference(L0_attn_x, L0_attn_norm_w, L0_attn_in_proj_w, L0_attn_conv_w, L0_attn_conv_b, L0_attn_x_proj_w, L0_attn_dt_w, L0_attn_dt_b, L0_attn_A_log, L0_attn_D_param, L0_attn_out_proj_w, L0_ffn_router_weight, L0_ffn_e_bias, L0_ffn_Wg, L0_ffn_Wu, L0_ffn_Wd, L0_ffn_sWg, L0_ffn_sWu, L0_ffn_sWd):

    def _L0_attn_ref(x, norm_w, in_proj_w, conv_w, conv_b, x_proj_w, dt_w, dt_b, A_log, D_param, out_proj_w):
        import jax, jax.numpy as jnp
        import numpy as np
        D_MODEL = 256
        STATE = 16
        KCONV = 4
        EXPAND = 2
        D_INNER = D_MODEL * EXPAND
        EPS = 1e-05

        def _silu(v):
            return v * jax.nn.sigmoid(v)
        residual = x
        xn = x * jax.lax.rsqrt(jnp.mean(x * x, axis=-1, keepdims=True) + EPS) * norm_w
        xz = jnp.einsum('bld,ed->ble', xn, in_proj_w)
        x_inner, z = jnp.split(xz, 2, axis=-1)
        xc = jnp.transpose(x_inner, (0, 2, 1))
        xc = jax.lax.conv_general_dilated(xc, conv_w, window_strides=(1,), padding=[(KCONV - 1, 0)], dimension_numbers=('NCH', 'OIH', 'NCH'), feature_group_count=D_INNER)
        xc = xc + conv_b[None, :, None]
        xc = _silu(jnp.transpose(xc, (0, 2, 1)))
        x_ssm = jnp.einsum('bld,ed->ble', xc, x_proj_w)
        dt = jax.nn.softplus(x_ssm[..., -1:] * dt_w[:, 0] + dt_b)
        B_p = x_ssm[..., :STATE]
        C_p = x_ssm[..., STATE:2 * STATE]
        A = -jnp.exp(A_log)
        batch = x.shape[0]
        h0 = jnp.zeros((batch, D_INNER, STATE), x.dtype)

        def step(h, inp):
            dt_t, B_t, C_t, u_t = inp
            dA = jnp.exp(dt_t[..., None] * A)
            h = dA * h + (dt_t * u_t)[..., None] * B_t[:, None, :]
            y_t = jnp.sum(h * C_t[:, None, :], axis=-1) + D_param * u_t
            return (h, y_t)
        seq_first = lambda a: jnp.swapaxes(a, 0, 1)
        _, ys = jax.lax.scan(step, h0, (seq_first(dt), seq_first(B_p), seq_first(C_p), seq_first(xc)))
        y = jnp.swapaxes(ys, 0, 1)
        y = y * _silu(z)
        return jnp.einsum('ble,de->bld', y, out_proj_w) + residual

    def _L0_ffn_ref(hidden_states, router_weight, e_bias, Wg, Wu, Wd, sWg, sWu, sWd):
        import jax, jax.numpy as jnp
        import numpy as np
        E = 32
        D = 256
        I = 176
        NG = 8
        TKG = 4
        TOPK = 8
        SCALE = 2.5
        SI = I * 2

        def _route(x, router_weight, e_bias):
            T = x.shape[0]
            scores = jax.nn.sigmoid(x @ router_weight.T)
            sfc = scores + e_bias[None, :]
            grp = sfc.reshape(T, NG, E // NG)
            top2, _ = jax.lax.top_k(grp, 2)
            group_scores = top2.sum(-1)
            _, gidx = jax.lax.top_k(group_scores, TKG)
            gmask = jnp.zeros((T, NG), sfc.dtype).at[jnp.arange(T)[:, None], gidx].set(1.0)
            smask = jnp.repeat(gmask, E // NG, axis=1)
            masked = jnp.where(smask > 0, sfc, 0.0)
            _, topk_idx = jax.lax.top_k(masked, TOPK)
            topk_w = jnp.take_along_axis(scores, topk_idx, axis=1)
            topk_w = topk_w / (topk_w.sum(-1, keepdims=True) + 1e-20)
            topk_w = topk_w * SCALE
            combine = jnp.zeros((T, E), scores.dtype).at[jnp.arange(T)[:, None], topk_idx].add(topk_w)
            return combine
        orig = hidden_states.shape
        x = hidden_states.reshape(-1, orig[-1])
        combine = _route(x, router_weight, e_bias)

        def body(acc, ws):
            wg, wu, wd, cw = ws
            h = jax.nn.silu(x @ wg.T) * (x @ wu.T)
            return (acc + cw[:, None] * (h @ wd.T), None)
        acc, _ = jax.lax.scan(body, jnp.zeros_like(x), (Wg, Wu, Wd, combine.T))
        shared = jax.nn.silu(x @ sWg.T) * (x @ sWu.T) @ sWd.T
        return (acc + shared).reshape(orig)
    x = L0_attn_x
    x = x + _layernorm(_L0_attn_ref(_layernorm(x, axis=-1), L0_attn_norm_w, L0_attn_in_proj_w, L0_attn_conv_w, L0_attn_conv_b, L0_attn_x_proj_w, L0_attn_dt_w, L0_attn_dt_b, L0_attn_A_log, L0_attn_D_param, L0_attn_out_proj_w), axis=-1)
    x = x + _layernorm(_L0_ffn_ref(_layernorm(x, axis=-1), L0_ffn_router_weight, L0_ffn_e_bias, L0_ffn_Wg, L0_ffn_Wu, L0_ffn_Wd, L0_ffn_sWg, L0_ffn_sWu, L0_ffn_sWd), axis=-1)
    return x

_drawn_inputs = setup_inputs


def setup_inputs(seed=0):
    import zlib

    import numpy as np

    out = dict(_drawn_inputs(seed))
    spreads = {'L0_attn_norm_w': (1.0, 0.6),
     'L0_attn_conv_b': (0.0, 0.8),
     'L0_attn_dt_b': (0.0, 0.8),
     'L0_attn_D_param': (1.0, 0.6),
     'L0_ffn_e_bias': (0.0, 0.1)}
    factors = {'L0_attn_in_proj_w': 7.131,
     'L0_attn_conv_w': 8.0,
     'L0_attn_x_proj_w': 8.0,
     'L0_attn_dt_w': 8.0,
     'L0_attn_A_log': 8.0,
     'L0_attn_out_proj_w': 5.229}
    for name, (base, spread) in spreads.items():
        noise = np.random.default_rng([zlib.crc32(name.encode()), seed]).standard_normal(out[name].shape)
        drawn = base * np.exp(spread * noise) if base else spread * noise
        out[name] = jnp.asarray(drawn.astype(out[name].dtype))
    for name, factor in factors.items():
        out[name] = (out[name] * factor).astype(out[name].dtype)
    return out
```

```python
from contextlib import ExitStack

import concourse.bass as bass
import numpy as np
from concourse import mybir

ALU = mybir.AluOpType
ACT = mybir.ActivationFunctionType
AX = mybir.AxisListType
F32 = mybir.dt.float32
F32R = mybir.dt.float32r
BF16 = mybir.dt.bfloat16

P = 128
BATCH, SEQ, D = 4, 256, 256
TOK = BATCH * SEQ
NT = TOK // P
HALF = 512
NH = TOK // HALF
TPH = NT // NH
KD = D // P
DI = 512
NQ = DI // P
NS = 16
KC = 4
NX = 2 * NS + 1
EPS = 1e-5
E, I, SI = 32, 176, 352
NG, TKG, TOPK = 8, 4, 8
GE = E // NG
SCALE = 2.5
NB = (E * I + SI + P - 1) // P
NBE = E * I // P
assert NBE * P == E * I
WB = 2 * KD * P + D
RING = 3
CW = 3 * E + 1

GATE_BANK, UP_BANK, CW_BANK = (4, 7), 5, 6

OFF_NW = 0
OFF_CONV = OFF_NW + KD
OFF_CB = OFF_CONV + NQ * KC
OFF_XP = OFF_CB + NQ
OFF_DTW = OFF_XP + NQ * NX
OFF_DTB = OFF_DTW + NQ
OFF_AL = OFF_DTB + NQ
OFF_DP = OFF_AL + NQ * NS
OFF_RW = OFF_DP + NQ
NPAR = OFF_RW + KD * E


def build(nc, x, w_in, params, w_out, e_bias, w_moe, ident_d, sel_row_d, sel_c_d, sel_cw_d, out):
    with ExitStack() as ctx:
        def sb(name, shape, dt=F32):
            return ctx.enter_context(nc.sbuf_tensor(name, shape, dt))

        def sem(name):
            return ctx.enter_context(nc.semaphore(name))

        x_sb = sb("x_sb", [P, NT, D])
        x1 = sb("x1", [P, NT, D])
        wout = sb("wout", [P, NQ, D])
        par = sb("par", [P, NPAR])
        idn = sb("idn", [P, P])
        eb = sb("eb", [P, E])
        stats = sb("stats", [P, NT, 6])
        mv = sb("mv", [P, NT, 2])
        sd = sb("sd", [P, NT])
        rstd = sb("rstd", [P, NT])
        ssq = sb("ssq", [P, NT])
        rms = sb("rms", [P, NT])
        rrms = sb("rrms", [P, NT])
        a_sb = sb("a_sb", [P, NQ * NS])
        xc = sb("xc", [P, NQ, TOK])
        sz = sb("sz", [P, NQ, TOK])
        ddiag = sb("ddiag", [P, NQ, P])
        selrow = sb("selrow", [NX, P])
        selc = sb("selc", [3 * 2 * NS, NS, P], BF16)

        with ExitStack() as early:
            def sbe(name, shape, dt=F32):
                return early.enter_context(nc.sbuf_tensor(name, shape, dt))

            junk = sbe("junk", [P, D])
            xn = sbe("xn", [P, NT, D])
            xnT = sbe("xnT", [P, KD, TOK])
            win = sbe("win", [P, KD, 2 * DI])
            cacc = sbe("cacc", [P, 2, TOK])

        with ExitStack() as scanning:
            def sbs(name, shape, dt=F32):
                return scanning.enter_context(nc.sbuf_tensor(name, shape, dt))

            bbc = sbs("bbc", [P, NS, TOK])
            xs = sbs("xs", [NX, TOK])
            xdt = sbs("xdt", [P, TOK])
            c3 = sbs("c3", [3 * 2 * NS, TOK], BF16)
            sp_abs = sbs("sp_abs", [P, TOK])
            sp_exp = sbs("sp_exp", [P, TOK])
            sp_w = sbs("sp_w", [P, TOK])
            sp_relu = sbs("sp_relu", [P, TOK])
            dt = sbs("dt", [P, 2, TOK])
            dtu = sbs("dtu", [P, 2, TOK])
            dbu = sbs("dbu", [P, 4, TOK])
            with ExitStack() as splitting:
                cmid = splitting.enter_context(nc.sbuf_tensor("cmid", [2 * NS, TOK], BF16))
                cres = splitting.enter_context(nc.sbuf_tensor("cres", [2 * NS, 2, TOK], F32))
            hs = sbs("hs", [P, 4, TOK])

        xn2 = sb("xn2", [P, NT, D])
        x2 = sb("x2", [P, NT, D])
        selcw = sb("selcw", [CW, NB, P], BF16)
        xfh = sb("xfh", [P, KD, TOK], F32R)
        xfl = sb("xfl", [P, KD, TOK], F32R)
        cw3 = sb("cw3", [CW, TOK], BF16)
        cwmid = sb("cwmid", [E, TOK], BF16)
        cwres = sb("cwres", [E, 2, TOK])
        rt = sb("rt", [P, 10, NT * E])
        wraw = sb("wraw", [P, RING, WB])
        wh = sb("wh", [P, RING, WB], F32R)
        wl = sb("wl", [P, RING, WB], F32R)
        sg = sb("sg", [P, 2, HALF])
        m1 = sb("m1", [P, 2, HALF])
        hbuf = sb("hbuf", [P, 2, HALF])
        hh = sb("hh", [P, 2, HALF], F32R)
        hl = sb("hl", [P, 2, HALF], F32R)
        scores = rt[:, 8, :]
        sfc = rt[:, 9, :]
        accT = xc
        ps = ctx.enter_context(nc.psum_tensor("ps", [P, 8, HALF], F32))

        def pair(k):
            return ps[:, 2 * k:2 * k + 2, :].rearrange("p a b -> p (a b)")

        b_scratch = nc.dram_tensor("b_scratch", [NS, TOK], F32, kind="Internal").ap()

        s_x = [sem(f"x_loaded{g}") for g in range(NH)]
        s_par = sem("params_loaded")
        s_id = sem("ident_loaded")
        s_win = sem("w_in_loaded")
        s_wout = sem("w_out_loaded")
        s_sel = sem("selectors_loaded")
        s_selcw = sem("cw_selector_loaded")
        s_bw = sem("b_rows_stored")
        s_bbc = [sem(f"b_broadcast{k}") for k in range(4)]
        s_out = sem("out_stored")

        dve_step = sem("dve_step")
        s_var = sem("variance_ready")
        s_sd = sem("deviation_ready")
        s_x1 = sem("x1_ready")
        s_ss = sem("square_sums_ready")
        s_ms = sem("mean_square_ready")
        s_rms = sem("rms_ready")
        s_rr = sem("inverse_rms_ready")
        s_xn = sem("xn_ready")
        s_tp = sem("transposed")
        s_xnT = sem("xnT_ready")
        s_inp = sem("in_proj_done")
        s_tap = sem("first_tap_ready")
        s_conv = sem("conv_ready")
        s_xc = sem("xc_ready")
        s_z = sem("silu_z_ready")
        s_xp = sem("x_proj_done")
        s_xs = sem("xs_ready")
        s_dtb = sem("dt_row_broadcast")
        s_xdt = sem("xdt_ready")
        s_c3 = sem("c_parts_ready")
        s_a = sem("a_ready")
        s_ea = sem("exp_a_log_ready")
        s_zero = sem("first_columns_zeroed")
        act_sp = sem("softplus_step")
        s_cor = sem("softplus_correction_ready")
        s_sum = sem("softplus_sum_ready")
        s_dt = sem("dt_ready")
        s_dtu = sem("dtu_ready")
        s_dd = sem("d_diagonal_ready")
        s_da = sem("decay_ready")
        s_dbu = sem("dbu_ready")
        s_scan = sem("scan_done")
        s_cb = sem("c_broadcast_done")
        s_hc = sem("hc_ready")
        s_y = sem("y_added")
        s_yz = sem("yz_ready")
        s_o = sem("out_proj_done")
        s_r = sem("residual_sum_ready")
        s_sd2 = sem("deviation2_ready")
        s_sd3 = sem("deviation3_ready")
        s_var2 = sem("variance2_ready")
        s_var3 = sem("variance3_ready")
        s_xf = sem("xf_ready")
        s_tp2 = sem("xf_transposed")
        s_xh = sem("xf_parts_ready")
        s_lg = sem("logits_done")
        s_sc = sem("scores_ready")
        s_cmb = sem("combine_ready")
        s_cT = sem("combine_transposed")
        s_cw3 = sem("combine_parts_ready")
        s_g = sem("gate_done")
        s_u = sem("up_done")
        s_c = sem("cw_broadcast_done")
        s_d = sem("down_done")
        s_sg = sem("silu_gate_ready")
        s_m1 = sem("gated_ready")
        s_h = sem("h_ready")
        s_hh = sem("h_high_ready")
        s_hl = sem("h_low_ready")
        s_wld = [sem(f"expert_weights_loaded{k}") for k in range(RING)]
        s_wh = sem("w_high_ready")
        s_wl = sem("w_low_ready")
        s_acc = sem("sums_copied")
        s_tp3 = sem("sums_transposed")
        s_var4 = sem("variance4_ready")
        s_sd4 = sem("deviation4_ready")
        s_fin = sem("final_ready")

        block = ctx.enter_context(nc.Block())

        @block.sync
        def _(sp):
            xt = x.rearrange("b s d -> (b s) d").rearrange("(t p) d -> p t d", p=P)
            for g in range(NH):
                sp.dma_start(x_sb[:, g * TPH:(g + 1) * TPH, :], xt[:, g * TPH:(g + 1) * TPH, :]).then_inc(s_x[g], 16)
            sp.dma_start(idn[:], ident_d).then_inc(s_id, 16)
            sp.dma_start(par[:], params).then_inc(s_par, 16)
            sp.dma_start(win[:], w_in).then_inc(s_win, 16)
            sp.dma_start(selrow[:], sel_row_d).then_inc(s_sel, 16)
            sp.dma_start(selc[:], sel_c_d).then_inc(s_sel, 16)
            sp.dma_start(wout[:], w_out).then_inc(s_wout, 16)
            sp.dma_start(eb[:], e_bias.rearrange("(a e) -> a e", a=1).to_broadcast([P, E])).then_inc(s_wout, 16)
            sp.wait_ge(s_xs, 1)
            sp.dma_start(b_scratch, xs[0:NS, :]).then_inc(s_bw, 16)
            sp.wait_ge(s_bw, 16)
            for k in range(4):
                src = b_scratch[4 * k:4 * k + 4, :].rearrange("(a n) t -> a n t", a=1).to_broadcast([P, 4, TOK])
                sp.dma_start(bbc[:, 4 * k:4 * k + 4, :], src).then_inc(s_bbc[k], 16)
            sp.wait_ge(s_yz, NQ)
            sp.dma_start(selcw[:], sel_cw_d).then_inc(s_selcw, 16)
            for b in range(RING):
                sp.dma_start(wraw[:, b, :], w_moe[b]).then_inc(s_wld[b], 16)
            with sp.Fori(1, NB // RING) as m:
                for s in range(RING):
                    sp.wait_ge(s_wl, RING * m + (s - RING + 1))
                    sp.dma_start(wraw[:, s, :], w_moe[bass.ds(RING * m + s, 1), :, :].rearrange("a p w -> p (a w)")).then_inc(s_wld[s], 16)
            for b in range(NB - NB % RING, NB):
                sp.wait_ge(s_wl, b - RING + 1)
                sp.dma_start(wraw[:, b % RING, :], w_moe[b]).then_inc(s_wld[b % RING], 16)
            ot = out.rearrange("b s d -> (b s) d").rearrange("(t p) d -> p t d", p=P)
            for g in range(NH):
                sp.wait_ge(s_fin, TPH * (g + 1))
                sp.dma_start(ot[:, g * TPH:(g + 1) * TPH, :], xn2[:, g * TPH:(g + 1) * TPH, :]).then_inc(s_out, 16)
            sp.wait_ge(s_out, 16 * NH)

        @block.tensor
        def _(pe):
            pe.wait_ge(s_id, 16)
            for g in range(NH):
                for t in range(g * TPH, (g + 1) * TPH):
                    pe.wait_ge(s_xn, t + 1)
                    for k in range(KD):
                        mm = nc.tensor.transpose(ps[:, 2 * g + k, (t % TPH) * P:(t % TPH + 1) * P],
                                                 xn[:, t, k * P:(k + 1) * P], idn[:])
                mm.then_inc(s_tp, 1)

            def in_proj(j):
                slot = (2, 3, 0)[j % 3]
                for h in range(NH):
                    if j == 0:
                        pe.wait_ge(s_xnT, KD * (h + 1))
                    for k in range(KD):
                        mm = nc.tensor.matmul(ps[:, 2 * slot + h, :], win[:, k, j * P:(j + 1) * P],
                                              xnT[:, k, h * HALF:(h + 1) * HALF], start=(k == 0), stop=(k == KD - 1))
                mm.then_inc(s_inp, 1)

            def x_proj(j):
                pe.wait_ge(s_xc, j + 1)
                for h in range(NH):
                    mm = nc.tensor.matmul(ps[0:NX, 2 + h, :], par[:, OFF_XP + j * NX:OFF_XP + (j + 1) * NX],
                                          xc[:, j, h * HALF:(h + 1) * HALF], start=(j == 0), stop=(j == NQ - 1))
                mm.then_inc(s_xp, 1)

            pe.wait_ge(s_win, 16)
            pe.wait_ge(s_par, 16)
            for j in range(NQ):
                if j == 3:
                    pe.wait_ge(s_conv, 1)
                in_proj(j)
            for j in range(NQ):
                if j < 2:
                    pe.wait_ge(s_conv, j + 2)
                elif j == 2:
                    pe.wait_ge(s_conv, 4)
                else:
                    pe.wait_ge(s_z, 1)
                in_proj(NQ + j)
                x_proj(j)
            pe.wait_ge(s_xs, 1)
            pe.wait_ge(s_sel, 32)
            for h in range(NH):
                mm = nc.tensor.matmul(ps[:, 2 + h, :], selrow[:], xs[:, h * HALF:(h + 1) * HALF], start=True, stop=True)
            mm.then_inc(s_dtb, 1)

            def c_bcast(n, wait):
                pe.wait_ge(*wait)
                for h in range(NH):
                    lhs = selc[:, n, :] if not in_loop(n) else selc[:, bass.ds(n, 1), :].rearrange("p a b -> p (a b)")
                    mm = nc.tensor.matmul(ps[:, 4 + h, :], lhs, c3[:, h * HALF:(h + 1) * HALF], start=True, stop=True)
                mm.then_inc(s_cb, 1)

            def y_start(q):
                pe.wait_ge(s_dd, 1)
                if q > 0:
                    pe.wait_ge(s_yz, q)
                for h in range(NH):
                    nc.tensor.matmul(ps[:, 6 + h, :], ddiag[:, q, :], xc[:, q, h * HALF:(h + 1) * HALF],
                                     start=True, stop=False)

            def y_add(slot, wait, last):
                pe.wait_ge(*wait)
                for h in range(NH):
                    mm = nc.tensor.matmul(ps[:, 6 + h, :], idn[:], hs[:, slot, h * HALF:(h + 1) * HALF],
                                          start=False, stop=last)
                mm.then_inc(s_y, 1)

            pe.wait_ge(s_c3, 1)
            pe.wait_ge(s_z, NQ)
            for q in range(NQ):
                for k in range(4):
                    u = NS * q + k
                    c_bcast(k, (s_hc, u) if u else (s_c3, 1))
                    if k == 1:
                        y_start(q)
                    if u:
                        y_add((k - 1) % 4, (s_hc, u), last=(k == 0))
                with pe.Fori(1, 4) as j:
                    for k in range(4):
                        c_bcast(4 * j + k, (s_hc, 4 * j + (NS * q + k)))
                        y_add((k - 1) % 4, (s_hc, 4 * j + (NS * q + k)), last=False)
            y_add(3, (s_hc, NS * NQ), last=True)

            pe.wait_ge(s_wout, 32)
            pe.wait_ge(s_yz, NQ)
            for t in range(NT):
                for q in range(NQ):
                    mm = nc.tensor.matmul(ps[:, t, 0:D], sz[:, q, t * P:(t + 1) * P], wout[:, q, :],
                                          start=(q == 0), stop=(q == NQ - 1))
                mm.then_inc(s_o, 1)
            for g in range(NH):
                for t in range(g * TPH, (g + 1) * TPH):
                    pe.wait_ge(s_xf, t + 1)
                    for k in range(KD):
                        mm = nc.tensor.transpose(ps[:, 2 * g + k, (t % TPH) * P:(t % TPH + 1) * P],
                                                 xn2[:, t, k * P:(k + 1) * P], idn[:])
                mm.then_inc(s_tp2, 1)
            rw = par[:, OFF_RW:OFF_RW + KD * E].rearrange("p (k e) -> p k e", k=KD)
            pe.wait_ge(s_xh, 2 * KD * NH)
            for t in range(NT):
                for k in range(KD):
                    for part in (xfh, xfl):
                        mm = nc.tensor.matmul(ps[:, 4, t * E:(t + 1) * E], part[:, k, t * P:(t + 1) * P].bitcast(F32),
                                              rw[:, k, :], start=(k == 0 and part is xfh), stop=(k == KD - 1 and part is xfl))
            mm.then_inc(s_lg, 1)
            pe.wait_ge(s_cmb, 1)
            for t in range(NT):
                mm = nc.tensor.transpose(ps[0:E, 6 + t // TPH, (t % TPH) * P:(t % TPH + 1) * P],
                                         rt[:, 0, t * E:(t + 1) * E], idn[:])
            mm.then_inc(s_cT, 1)

            def three(dst, w_cols, rhs_h, rhs_l, slot, start, stop):
                for n, (w, r) in enumerate(((wh, rhs_h), (wh, rhs_l), (wl, rhs_h))):
                    mm = nc.tensor.matmul(dst, w[:, slot, w_cols], r, start=(start and n == 0), stop=(stop and n == 2),
                                          skip_group_check=True)
                return mm

            def up_part(half, slot, b, step, first):
                hc_ = slice(half * HALF, (half + 1) * HALF)
                pe.wait_ge(s_wl, b + 1)
                if not (first and True):
                    pe.wait_ge(s_sg, step - 1)
                for k in range(KD):
                    mm = three(ps[:, GATE_BANK[half], :], slice(k * P, (k + 1) * P), xfh[:, k, hc_], xfl[:, k, hc_], slot,
                               k == 0, k == KD - 1)
                mm.then_inc(s_g, 1)
                if not (first and half == 0):
                    pe.wait_ge(s_m1, step)
                for k in range(KD):
                    mm = three(ps[:, UP_BANK, :], slice((KD + k) * P, (KD + k + 1) * P), xfh[:, k, hc_], xfl[:, k, hc_], slot,
                               k == 0, k == KD - 1)
                mm.then_inc(s_u, 1)
                if not (first and half == 0):
                    pe.wait_ge(s_h, step)
                else:
                    pe.wait_ge(s_cw3, 1)
                lhs = selcw[:, b, :] if isinstance(b, int) else selcw[:, bass.ds(b, 1), :].rearrange("p a b -> p (a b)")
                nc.tensor.matmul(ps[:, CW_BANK, :], lhs, cw3[:, hc_], start=True, stop=True).then_inc(s_c, 1)

            def down_part(half, slot, step_after, first, last):
                pe.wait_ge(s_hl, step_after)
                for dblk in range(KD):
                    mm = three(ps[:, 2 * dblk + half, :], slice(2 * KD * P + dblk * P, 2 * KD * P + (dblk + 1) * P),
                               hh[:, half, :], hl[:, half, :], slot, first, last)
                mm.then_inc(s_d, 1)

            pe.wait_ge(s_sc, 1)
            pe.wait_ge(s_selcw, 16)
            for b in range(RING):
                for half in range(NH):
                    up_part(half, b, b, 2 * b + half, b == 0)
                    if b or half:
                        prev = 2 * b + half - 1
                        down_part(prev % 2, prev // 2, prev + 1, prev < 2, False)
            with pe.Fori(1, NB // RING) as m:
                for s in range(RING):
                    for half in range(NH):
                        up_part(half, s, RING * m + s, 2 * RING * m + (2 * s + half), False)
                        prev = 2 * s + half - 1
                        down_part(prev % 2, (prev // 2) % RING, 2 * RING * m + (prev + 1), False, False)
            for b in range(NB - NB % RING, NB):
                for half in range(NH):
                    up_part(half, b % RING, b, 2 * b + half, False)
                    prev = 2 * b + half - 1
                    down_part(prev % 2, (prev // 2) % RING, prev + 1, False, prev == 2 * NB - 2)
            down_part(1, (NB - 1) % RING, 2 * NB, False, True)
            for h in range(NH):
                pe.wait_ge(s_acc, KD * (h + 1))
                for t in range(h * TPH, (h + 1) * TPH):
                    for k in range(KD):
                        mm = nc.tensor.transpose(ps[:, (4 + t) % 8, k * P:(k + 1) * P],
                                                 accT[:, k, t * P:(t + 1) * P], idn[:])
                    mm.then_inc(s_tp3, 1)

        @block.scalar
        def _(act):
            act.wait_ge(s_par, 16)
            nc.scalar.activation(a_sb[:], par[:, OFF_AL:OFF_AL + NQ * NS], ACT.Exp).then_inc(s_ea, 1)
            for g in range(NH):
                ts = slice(g * TPH, (g + 1) * TPH)
                act.wait_ge(s_var, g + 1)
                nc.scalar.activation(sd[:, ts], mv[:, ts, 1], ACT.Sqrt).then_inc(s_sd, 1)
                for t in range(g * TPH, (g + 1) * TPH):
                    act.wait_ge(s_x1, t + 1)
                    if t:
                        act.wait_ge(s_ss, t)
                    nc.scalar.activation(junk[:], x1[:, t, :], ACT.Square, accum_out=ssq[:, t:t + 1]).then_inc(s_ss, 1)
                act.wait_ge(s_ms, g + 1)
                nc.scalar.activation(rms[:, ts], ssq[:, ts], ACT.Sqrt).then_inc(s_rms, 1)
                for t in range(g * TPH, (g + 1) * TPH):
                    act.wait_ge(s_rr, g + 1)
                    nc.scalar.activation(xn[:, t, :], x1[:, t, :], ACT.Copy, scale=rrms[:, t:t + 1]).then_inc(s_xn, 1)

            def first_tap(j):
                slot = (2, 3, 0)[j % 3]
                act.wait_ge(s_inp, j + 1)
                if j >= 2:
                    act.wait_ge(s_xc, j - 1)
                nc.scalar.activation(cacc[:, j % 2, :], pair(slot), ACT.Identity,
                                     scale=par[:, OFF_CONV + j * KC + KC - 1:OFF_CONV + j * KC + KC],
                                     bias=par[:, OFF_CB + j:OFF_CB + j + 1]).then_inc(s_tap, 1)

            def silu_xc(j):
                act.wait_ge(s_conv, j + 1)
                nc.scalar.activation(xc[:, j, :], cacc[:, j % 2, :], ACT.Silu).then_inc(s_xc, 1)

            def silu_z(j):
                act.wait_ge(s_inp, NQ + j + 1)
                nc.scalar.activation(sz[:, j, :], pair((2, 3, 0)[(NQ + j) % 3]), ACT.Silu).then_inc(s_z, 1)

            first_tap(0)
            first_tap(1)
            for j in range(NQ):
                silu_xc(j)
                if j + 2 < NQ:
                    first_tap(j + 2)
            for j in range(NQ):
                silu_z(j)
            act.wait_ge(s_xp, NQ)
            nc.scalar.copy(xs[:], ps[0:NX, 2:4, :].rearrange("p a b -> p (a b)")).then_inc(s_xs, 1)
            act.wait_ge(s_dtb, 1)
            nc.scalar.copy(xdt[:], pair(1)).then_inc(s_xdt, 1)

            def softplus(q):
                sc, bi = par[:, OFF_DTW + q:OFF_DTW + q + 1], par[:, OFF_DTB + q:OFF_DTB + q + 1]
                n = 5 * q
                if q:
                    act.wait_ge(s_dt, q)
                act.wait_ge(s_xdt, 1)
                nc.scalar.activation(sp_abs[:], xdt[:], ACT.Abs, scale=sc, bias=bi).then_inc(act_sp, 1)
                nc.scalar.activation(sp_relu[:], xdt[:], ACT.Relu, scale=sc, bias=bi).then_inc(act_sp, 1)
                act.wait_ge(act_sp, n + 2)
                nc.scalar.activation(sp_exp[:], sp_abs[:], ACT.Exp, scale=-1.0).then_inc(act_sp, 1)
                act.wait_ge(act_sp, n + 3)
                nc.scalar.activation(sp_w[:], sp_exp[:], ACT.Identity, bias=1.0).then_inc(act_sp, 1)
                act.wait_ge(act_sp, n + 4)
                nc.scalar.activation(sp_abs[:], sp_w[:], ACT.Ln).then_inc(act_sp, 1)

            def decay(q, n, slot, wait):
                act.wait_ge(*wait)
                dst = pair(slot).rearrange("p (b s) -> p b s", b=BATCH)[:, :, 1:SEQ]
                src = dt[:, q % 2, :].rearrange("p (b s) -> p b s", b=BATCH)[:, :, 1:SEQ]
                sc = a_sb[:, bass.ds(n + NS * q, 1)] if in_loop(n) else a_sb[:, NS * q + n:NS * q + n + 1]
                nc.scalar.activation(dst, src, ACT.Exp, scale=sc).then_inc(s_da, 1)

            softplus(0)
            act.wait_ge(s_zero, 1)
            act.wait_ge(s_a, 1)
            for q in range(NQ):
                act.wait_ge(s_dt, q + 1)
                for k in range(4):
                    u = NS * q + k
                    decay(q, k, k % 2, (s_scan, u - 1) if u >= 2 else (s_zero, 1))
                    if k == 1 and q + 1 < NQ:
                        softplus(q + 1)
                with act.Fori(1, 4) as j:
                    for k in range(4):
                        decay(q, 4 * j + k, k % 2, (s_scan, 4 * j + (NS * q + k - 1)))

            for n, (sv, ss) in enumerate(((s_var2, s_sd2), (s_var3, s_sd3))):
                for g in range(NH):
                    ts = slice(g * TPH, (g + 1) * TPH)
                    act.wait_ge(sv, g + 1)
                    nc.scalar.activation(sd[:, ts], mv[:, ts, 1], ACT.Sqrt).then_inc(ss, 1)
            act.wait_ge(s_lg, 1)
            nc.scalar.activation(scores, ps[:, 4, 0:NT * E], ACT.Sigmoid).then_inc(s_sc, 1)

            def w_high(b, slot, wait_load, wait_down):
                act.wait_ge(s_wld[slot], wait_load)
                if wait_down is not None:
                    act.wait_ge(s_d, wait_down)
                nc.scalar.copy(wh[:, slot, :], wraw[:, slot, :]).then_inc(s_wh, 1)

            def act_step(half, step, first):
                act.wait_ge(s_g, step + 1)
                if not first:
                    act.wait_ge(s_m1, step - 1)
                nc.scalar.activation(sg[:, half, :], ps[:, GATE_BANK[half], :], ACT.Silu).then_inc(s_sg, 1)
                act.wait_ge(s_h, step + 1)
                if not first:
                    act.wait_ge(s_d, step - 1)
                nc.scalar.copy(hh[:, half, :], hbuf[:, half, :]).then_inc(s_hh, 1)

            w_high(0, 0, 16, None)
            for b in range(RING):
                act_step(0, 2 * b, b == 0)
                nb = b + 1
                w_high(nb, nb % RING, 16 * (nb // RING + 1), 2 * nb - 4 if nb >= RING else None)
                act_step(1, 2 * b + 1, b == 0)
            with act.Fori(1, NB // RING) as m:
                for s in range(RING):
                    act_step(0, 2 * RING * m + 2 * s, False)
                    w_high(None, (s + 1) % RING, 16 * m + 16 * ((s + 1) // RING + 1), 2 * RING * m + (2 * (s + 1) - 4))
                    act_step(1, 2 * RING * m + (2 * s + 1), False)
            for b in range(NB - NB % RING, NB):
                act_step(0, 2 * b, False)
                if b + 1 < NB:
                    nb = b + 1
                    w_high(nb, nb % RING, 16 * (nb // RING + 1), 2 * nb - 4)
                act_step(1, 2 * b + 1, False)
            for h in range(NH):
                act.wait_ge(s_d, 2 * NB - NH + h + 1)
                for k in range(KD):
                    nc.scalar.copy(accT[:, k, h * HALF:(h + 1) * HALF], ps[:, 2 * k + h, :]).then_inc(s_acc, 1)
            for g in range(NH):
                ts = slice(g * TPH, (g + 1) * TPH)
                act.wait_ge(s_var4, g + 1)
                nc.scalar.activation(sd[:, ts], mv[:, ts, 1], ACT.Sqrt).then_inc(s_sd4, 1)

        @block.gpsimd
        def _(pool):
            def softplus_sum(q):
                pool.wait_ge(act_sp, 5 * q + 5)
                nc.gpsimd.tensor_tensor(sp_relu[:], sp_relu[:], sp_abs[:], ALU.add).then_inc(s_sum, 1)

            def make_dtu(q):
                pool.wait_ge(s_dt, q + 1)
                if q >= 2:
                    pool.wait_ge(s_dbu, NS * (q - 1))
                nc.gpsimd.tensor_tensor(dtu[:, q % 2, :], dt[:, q % 2, :], xc[:, q, :], ALU.mult).then_inc(s_dtu, 1)

            def dbu_unit(q, n, slot, wait):
                if wait is not None:
                    pool.wait_ge(*wait)
                src = bbc[:, bass.ds(n, 1), :].rearrange("p a b -> p (a b)") if in_loop(n) else bbc[:, n, :]
                nc.gpsimd.tensor_tensor(dbu[:, slot, :], dtu[:, q % 2, :], src, ALU.mult).then_inc(s_dbu, 1)

            softplus_sum(0)
            make_dtu(0)
            for k in range(4):
                pool.wait_ge(s_bbc[k], 16)
            for q in range(NQ):
                pool.wait_ge(s_dtu, q + 1)
                for k in range(4):
                    u = NS * q + k
                    dbu_unit(q, k, k, (s_scan, u - 3) if u >= 4 else None)
                if q + 1 < NQ:
                    softplus_sum(q + 1)
                with pool.Fori(1, 4) as j:
                    for k in range(4):
                        dbu_unit(q, 4 * j + k, k, (s_scan, 4 * j + (NS * q + k - 3)))
                if q + 1 < NQ:
                    make_dtu(q + 1)

            def low(half, step, first):
                pool.wait_ge(s_hh, step + 1)
                if not first:
                    pool.wait_ge(s_d, step - 1)
                nc.gpsimd.tensor_tensor(hl[:, half, :], hbuf[:, half, :], hh[:, half, :].bitcast(F32),
                                        ALU.subtract).then_inc(s_hl, 1)

            for b in range(RING):
                for half in range(NH):
                    low(half, 2 * b + half, b == 0)
            with pool.Fori(1, NB // RING) as m:
                for s in range(RING):
                    for half in range(NH):
                        low(half, 2 * RING * m + (2 * s + half), False)
            for b in range(NB - NB % RING, NB):
                for half in range(NH):
                    low(half, 2 * b + half, False)

        @block.vector
        def _(dve):
            count = [0]

            def after(ins):
                count[0] += 1
                ins.then_inc(dve_step, 1)
                dve.wait_ge(dve_step, count[0])

            def moments(src, g, s_ready):
                for t in range(g * TPH, (g + 1) * TPH):
                    last = nc.vector.bn_stats(stats[:, t, :], src(t))
                after(last)
                for t in range(g * TPH, (g + 1) * TPH):
                    last = nc.vector.bn_aggr(mv[:, t, :], stats[:, t, :])
                after(last)
                ts = slice(g * TPH, (g + 1) * TPH)
                nc.vector.tensor_scalar(mv[:, ts, 1], mv[:, ts, 1], EPS, None, ALU.add).then_inc(s_ready, 1)

            def inverse(g, s_dev):
                ts = slice(g * TPH, (g + 1) * TPH)
                dve.wait_ge(s_dev, g + 1)
                after(nc.vector.reciprocal(rstd[:, ts], sd[:, ts]))

            def normed(dst, src, t):
                return nc.vector.tensor_scalar(dst, src, mv[:, t, 0:1], rstd[:, t:t + 1], ALU.subtract, ALU.mult)

            for g in range(NH):
                dve.wait_ge(s_x[g], 16)
                moments(lambda t: x_sb[:, t, :], g, s_var)
            dve.wait_ge(s_ea, 1)
            nc.vector.tensor_scalar(a_sb[:], a_sb[:], -1.0, None, ALU.mult).then_inc(s_a, 1)
            for g in range(NH):
                inverse(g, s_sd)
                for t in range(g * TPH, (g + 1) * TPH):
                    normed(x1[:, t, :], x_sb[:, t, :], t).then_inc(s_x1, 1)
                ts = slice(g * TPH, (g + 1) * TPH)
                dve.wait_ge(s_ss, TPH * (g + 1))
                nc.vector.tensor_scalar(ssq[:, ts], ssq[:, ts], 1.0 / D, EPS, ALU.mult, ALU.add).then_inc(s_ms, 1)
                dve.wait_ge(s_rms, g + 1)
                nc.vector.reciprocal(rrms[:, ts], rms[:, ts]).then_inc(s_rr, 1)
            for g in range(NH):
                dve.wait_ge(s_tp, g + 1)
                for k in range(KD):
                    nc.vector.tensor_scalar(xnT[:, k, g * HALF:(g + 1) * HALF], ps[:, 2 * g + k, :],
                                            par[:, OFF_NW + k:OFF_NW + k + 1], None, ALU.mult).then_inc(s_xnT, 1)
            for q in range(NQ):
                last = nc.vector.tensor_scalar(ddiag[:, q, :], idn[:], par[:, OFF_DP + q:OFF_DP + q + 1], None, ALU.mult)
            last.then_inc(s_dd, 1)
            for j in range(NQ):
                slot = (2, 3, 0)[j % 3]
                xi = pair(slot).rearrange("p (b s) -> p b s", b=BATCH)
                acc = cacc[:, j % 2, :].rearrange("p (b s) -> p b s", b=BATCH)
                dve.wait_ge(s_tap, j + 1)
                for shift in range(1, KC):
                    w = par[:, OFF_CONV + j * KC + KC - 1 - shift:OFF_CONV + j * KC + KC - shift]
                    ins = nc.vector.scalar_tensor_tensor(out=acc[:, :, shift:SEQ], in0=xi[:, :, 0:SEQ - shift], scalar=w,
                                                         in1=acc[:, :, shift:SEQ], op0=ALU.mult, op1=ALU.add)
                    if shift < KC - 1:
                        after(ins)
                    else:
                        ins.then_inc(s_conv, 1)

            def three_parts(dst, rows, src, mid, res):
                after(nc.vector.tensor_copy(dst[0:rows, :], src))
                after(nc.vector.tensor_tensor(res[:, 0, :], src, dst[0:rows, :], ALU.subtract))
                after(nc.vector.tensor_copy(mid, res[:, 0, :]))
                after(nc.vector.tensor_tensor(res[:, 1, :], res[:, 0, :], mid, ALU.subtract))
                nc.vector.tensor_copy(dst[rows:2 * rows, :], mid)
                return nc.vector.tensor_copy(dst[2 * rows:3 * rows, :], res[:, 1, :])

            dve.wait_ge(s_z, NQ)
            dve.wait_ge(s_xs, 1)
            dve.wait_ge(s_xdt, 1)
            nc.vector.memset(ps[:, 0:4, :].rearrange("p a (b s) -> p (a b) s", s=SEQ)[:, :, 0:1], 0.0).then_inc(s_zero, 1)
            three_parts(c3, 2 * NS, xs[0:2 * NS, :], cmid[:], cres).then_inc(s_c3, 1)

            def make_dt(q):
                dve.wait_ge(act_sp, 5 * q + 5)
                nc.vector.scalar_tensor_tensor(out=sp_w[:], in0=sp_w[:], scalar=1.0, in1=sp_exp[:],
                                               op0=ALU.subtract, op1=ALU.subtract).then_inc(s_cor, 1)
                dve.wait_ge(s_cor, q + 1)
                dve.wait_ge(s_sum, q + 1)
                if q >= 2:
                    dve.wait_ge(s_da, NS * (q - 1))
                    dve.wait_ge(s_dtu, q - 1)
                nc.vector.tensor_tensor(dt[:, q % 2, :], sp_relu[:], sp_w[:], ALU.subtract).then_inc(s_dt, 1)

            def scan(slot2, slot4, u, wait_y):
                dve.wait_ge(s_da, u + 1)
                dve.wait_ge(s_dbu, u + 1)
                if wait_y:
                    dve.wait_ge(s_y, u - 3)
                nc.vector.tensor_tensor_scan(hs[:, slot4, :], pair(slot2), dbu[:, slot4, :], 0.0,
                                             ALU.mult, ALU.add).then_inc(s_scan, 1)

            def times_c(slot4, u1):
                dve.wait_ge(s_scan, u1)
                dve.wait_ge(s_cb, u1)
                nc.vector.tensor_tensor(hs[:, slot4, :], hs[:, slot4, :], pair(2), ALU.mult).then_inc(s_hc, 1)

            def gate_y(q):
                dve.wait_ge(s_y, NS * (q + 1))
                nc.vector.tensor_tensor(sz[:, q, :], pair(3), sz[:, q, :], ALU.mult).then_inc(s_yz, 1)

            make_dt(0)
            dve.wait_ge(s_c3, 1)
            for q in range(NQ):
                for k in range(4):
                    u = NS * q + k
                    scan(k % 2, k, u, u >= 4)
                    if u:
                        times_c((k - 1) % 4, u)
                    if k == 1 and q:
                        gate_y(q - 1)
                with dve.Fori(1, 4) as j:
                    for k in range(4):
                        scan(k % 2, k, 4 * j + (NS * q + k), True)
                        times_c((k - 1) % 4, 4 * j + (NS * q + k))
                if q + 1 < NQ:
                    make_dt(q + 1)
            times_c(3, NS * NQ)
            gate_y(NQ - 1)

            def resid(t):
                dve.wait_ge(s_o, t + 1)
                return nc.vector.tensor_tensor(x1[:, t, :], ps[:, t, 0:D], x1[:, t, :], ALU.add)

            for g in range(NH):
                for t in range(g * TPH, (g + 1) * TPH):
                    last = resid(t)
                after(last)
                moments(lambda t: x1[:, t, :], g, s_var2)
            for g in range(NH):
                inverse(g, s_sd2)
                for t in range(g * TPH, (g + 1) * TPH):
                    last = normed(x1[:, t, :], x1[:, t, :], t)
                after(last)
                for t in range(g * TPH, (g + 1) * TPH):
                    last = nc.vector.tensor_tensor(x2[:, t, :], x_sb[:, t, :], x1[:, t, :], ALU.add)
                after(last)
            for g in range(NH):
                moments(lambda t: x2[:, t, :], g, s_var3)
            for g in range(NH):
                inverse(g, s_sd3)
                for t in range(g * TPH, (g + 1) * TPH):
                    normed(xn2[:, t, :], x2[:, t, :], t).then_inc(s_xf, 1)
            n = 0
            for g in range(NH):
                dve.wait_ge(s_tp2, g + 1)
                for k in range(KD):
                    cols = slice(g * HALF, (g + 1) * HALF)
                    nc.vector.tensor_copy(xfh[:, k, cols], ps[:, 2 * g + k, :]).then_inc(s_xh, 1)
                    n += 1
                    dve.wait_ge(s_xh, n)
                    nc.vector.tensor_tensor(xfl[:, k, cols], ps[:, 2 * g + k, :], xfh[:, k, cols].bitcast(F32),
                                            ALU.subtract).then_inc(s_xh, 1)
                    n += 1

            def w_low(slot, wait_high):
                dve.wait_ge(s_wh, wait_high)
                nc.vector.tensor_tensor(wl[:, slot, :], wraw[:, slot, :], wh[:, slot, :].bitcast(F32),
                                        ALU.subtract).then_inc(s_wl, 1)

            w_low(0, 1)
            def r3(a):
                return a.rearrange("p (t e) -> p t e", t=NT)

            def r4(a):
                return a.rearrange("p (t g e) -> p t g e", t=NT, g=NG)

            dve.wait_ge(s_wout, 32)
            dve.wait_ge(s_sc, 1)
            ebb = eb[:].rearrange("p (a e) -> p a e", a=1).to_broadcast([P, NT, E])
            after(nc.vector.tensor_tensor(r3(sfc), r3(scores), ebb, ALU.add))
            a, b, c, d = (r4(sfc)[:, :, :, i] for i in range(GE))
            W = NT * NG

            def v(slot, part):
                return rt[:, slot, part * W:(part + 1) * W].rearrange("p (t g) -> p t g", t=NT)

            nc.vector.tensor_tensor(v(1, 0), a, b, ALU.max)
            nc.vector.tensor_tensor(v(1, 1), a, b, ALU.min)
            nc.vector.tensor_tensor(v(1, 2), c, d, ALU.max)
            after(nc.vector.tensor_tensor(v(1, 3), c, d, ALU.min))
            nc.vector.tensor_tensor(v(2, 0), v(1, 0), v(1, 2), ALU.max)
            nc.vector.tensor_tensor(v(2, 1), v(1, 0), v(1, 2), ALU.min)
            after(nc.vector.tensor_tensor(v(2, 2), v(1, 1), v(1, 3), ALU.max))
            after(nc.vector.tensor_tensor(v(2, 3), v(2, 1), v(2, 2), ALU.max))
            after(nc.vector.tensor_tensor(v(3, 0), v(2, 0), v(2, 3), ALU.add))
            gs = v(3, 0)
            after(nc.vector.memset(v(3, 1), 0.0))
            for o in range(1, NG):
                nc.vector.tensor_tensor(v(3, 2)[:, :, 0:NG - o], gs[:, :, o:NG], gs[:, :, 0:NG - o], ALU.is_gt)
                after(nc.vector.tensor_tensor(v(3, 3)[:, :, o:NG], gs[:, :, 0:NG - o], gs[:, :, o:NG], ALU.is_ge))
                after(nc.vector.tensor_tensor(v(3, 1)[:, :, 0:NG - o], v(3, 1)[:, :, 0:NG - o],
                                              v(3, 2)[:, :, 0:NG - o], ALU.add))
                after(nc.vector.tensor_tensor(v(3, 1)[:, :, o:NG], v(3, 1)[:, :, o:NG], v(3, 3)[:, :, o:NG], ALU.add))
            after(nc.vector.tensor_scalar(v(2, 0), v(3, 1), float(TKG), None, ALU.is_lt))
            gm = rt[:, 2, 0:W].rearrange("p (t g e) -> p t g e", t=NT, e=1).to_broadcast([P, NT, NG, GE])
            after(nc.vector.tensor_tensor(r4(rt[:, 4, :]), r4(sfc), gm, ALU.mult))
            after(nc.vector.tensor_scalar(rt[:, 4, :], rt[:, 4, :], 0.0, None, ALU.add))
            for t in range(NT):
                last = nc.vector.max(rt[:, 5, t * TOPK:(t + 1) * TOPK], rt[:, 4, t * E:(t + 1) * E])
            after(last)
            for t in range(NT):
                last = nc.vector.match_replace(out=rt[:, 6, t * E:(t + 1) * E],
                                               in_to_replace=rt[:, 5, t * TOPK:(t + 1) * TOPK],
                                               in_values=rt[:, 4, t * E:(t + 1) * E], imm_value=-3.0e38)
            after(last)
            after(nc.vector.tensor_scalar(rt[:, 7, :], rt[:, 6, :], -3.0e38, None, ALU.is_equal))
            after(nc.vector.tensor_tensor(rt[:, 7, :], rt[:, 7, :], scores, ALU.mult))
            after(nc.vector.tensor_reduce(rt[:, 5, 0:NT], r3(rt[:, 7, :]), AX.X, ALU.add))
            after(nc.vector.tensor_scalar(rt[:, 5, 0:NT], rt[:, 5, 0:NT], 1e-20, None, ALU.add))
            after(nc.vector.reciprocal(rt[:, 5, NT:2 * NT], rt[:, 5, 0:NT]))
            inv = rt[:, 5, NT:2 * NT].rearrange("p (t e) -> p t e", e=1).to_broadcast([P, NT, E])
            after(nc.vector.tensor_tensor(r3(rt[:, 7, :]), r3(rt[:, 7, :]), inv, ALU.mult))
            nc.vector.tensor_scalar(rt[:, 0, :], rt[:, 7, :], SCALE, None, ALU.mult).then_inc(s_cmb, 1)
            nc.vector.memset(cw3[3 * E:CW, :], 1.0)
            dve.wait_ge(s_cT, 1)
            three_parts(cw3, E, ps[0:E, 6:8, :].rearrange("p a b -> p (a b)"), cwmid[:], cwres).then_inc(s_cw3, 1)

            def dve_step_i(half, step, first):
                dve.wait_ge(s_sg, step + 1)
                dve.wait_ge(s_u, step + 1)
                if not first:
                    dve.wait_ge(s_h, step - 1)
                nc.vector.tensor_tensor(m1[:, half, :], ps[:, UP_BANK, :], sg[:, half, :], ALU.mult).then_inc(s_m1, 1)
                dve.wait_ge(s_m1, step + 1)
                dve.wait_ge(s_c, step + 1)
                if not first:
                    dve.wait_ge(s_hl, step - 1)
                nc.vector.tensor_tensor(hbuf[:, half, :], ps[:, CW_BANK, :], m1[:, half, :], ALU.mult).then_inc(s_h, 1)

            for b_ in range(RING):
                dve_step_i(0, 2 * b_, b_ == 0)
                w_low((b_ + 1) % RING, b_ + 2)
                dve_step_i(1, 2 * b_ + 1, b_ == 0)
            with dve.Fori(1, NB // RING) as m:
                for s in range(RING):
                    dve_step_i(0, 2 * RING * m + 2 * s, False)
                    w_low((s + 1) % RING, RING * m + (s + 2))
                    dve_step_i(1, 2 * RING * m + (2 * s + 1), False)
            for b_ in range(NB - NB % RING, NB):
                dve_step_i(0, 2 * b_, False)
                if b_ + 1 < NB:
                    w_low((b_ + 1) % RING, b_ + 2)
                dve_step_i(1, 2 * b_ + 1, False)

            for g in range(NH):
                dve.wait_ge(s_tp3, TPH * (g + 1))
                moments(lambda t: ps[:, (4 + t) % 8, 0:D], g, s_var4)
            for g in range(NH):
                inverse(g, s_sd4)
                for t in range(g * TPH, (g + 1) * TPH):
                    last = normed(x1[:, t, :], ps[:, (4 + t) % 8, 0:D], t)
                after(last)
                for t in range(g * TPH, (g + 1) * TPH):
                    nc.vector.tensor_tensor(xn2[:, t, :], x2[:, t, :], x1[:, t, :], ALU.add).then_inc(s_fin, 1)


def in_loop(n):
    return not isinstance(n, int)


def kernel(**inputs):
    import concourse.bacc as bacc
    import ml_dtypes
    from concourse.bass_utils import run_bass_kernel_spmd as run

    def a(name):
        return np.asarray(inputs["L0_" + name])

    def rows(m, n):
        return m.reshape(n, P, -1).transpose(1, 0, 2)

    params = np.concatenate([
        rows(a("attn_norm_w"), KD).reshape(P, -1),
        rows(a("attn_conv_w").reshape(DI, KC), NQ).reshape(P, -1),
        rows(a("attn_conv_b"), NQ).reshape(P, -1),
        rows(a("attn_x_proj_w").T, NQ).reshape(P, -1),
        rows(a("attn_dt_w"), NQ).reshape(P, -1),
        rows(a("attn_dt_b"), NQ).reshape(P, -1),
        rows(a("attn_A_log"), NQ).reshape(P, -1),
        rows(a("attn_D_param"), NQ).reshape(P, -1),
        rows(a("ffn_router_weight").T, KD).reshape(P, -1),
    ], axis=1)
    pad = np.zeros((NB * P - E * I - SI, D), np.float32)

    def blocks(routed, shared):
        return np.concatenate([routed, shared, pad]).reshape(NB, P, D)

    def stationary(w):
        return w.reshape(NB, P, KD, P).transpose(0, 3, 2, 1).reshape(NB, P, KD * P)

    gate = stationary(blocks(a("ffn_Wg").reshape(E * I, D), a("ffn_sWg")))
    up = stationary(blocks(a("ffn_Wu").reshape(E * I, D), a("ffn_sWu")))
    down = blocks(a("ffn_Wd").transpose(0, 2, 1).reshape(E * I, D), a("ffn_sWd").T)
    sel_row = np.zeros((NX, P), np.float32)
    sel_row[NX - 1] = 1
    sel_c = np.zeros((3, 2 * NS, NS, P), ml_dtypes.bfloat16)
    for n in range(NS):
        sel_c[:, NS + n, n] = 1
    sel_cw = np.zeros((CW, NB * P), ml_dtypes.bfloat16)
    for e in range(E):
        for part in range(3):
            sel_cw[part * E + e, e * I:(e + 1) * I] = 1
    sel_cw[3 * E, E * I:] = 1
    arrays = {
        "x": a("attn_x"),
        "w_in": rows(a("attn_in_proj_w").T, KD),
        "params": params,
        "w_out": rows(a("attn_out_proj_w").T, NQ),
        "e_bias": a("ffn_e_bias"),
        "w_moe": np.concatenate([gate, up, down], axis=2),
        "ident": np.eye(P, dtype=np.float32),
        "sel_row": sel_row,
        "sel_c": sel_c.reshape(3 * 2 * NS, NS, P),
        "sel_cw": sel_cw.reshape(CW, NB, P),
    }
    arrays = {n: np.ascontiguousarray(v) for n, v in arrays.items()}
    nc = bacc.Bacc("TRN2", target_bir_lowering=False, num_devices=1)
    aps = [nc.dram_tensor(n, v.shape, mybir.dt.from_np(v.dtype), kind="ExternalInput").ap() for n, v in arrays.items()]
    aps.append(nc.dram_tensor("out", (BATCH, SEQ, D), F32, kind="ExternalOutput").ap())
    build(nc, *aps)
    return run(nc, [arrays], core_ids=[0]).results[0]["out"]
```

```python
from contextlib import ExitStack

import concourse.bass as bass
import numpy as np
from concourse import mybir

ALU = mybir.AluOpType
ACT = mybir.ActivationFunctionType
AX = mybir.AxisListType
F32 = mybir.dt.float32
F32R = mybir.dt.float32r
BF16 = mybir.dt.bfloat16

P = 128
BATCH, SEQ, D = 4, 256, 256
TOK = BATCH * SEQ
NT = TOK // P
HALF = 512
NH = TOK // HALF
TPH = NT // NH
KD = D // P
DI = 512
NQ = DI // P
NS = 16
KC = 4
NX = 2 * NS + 1
EPS = 1e-5
E, I, SI = 32, 176, 352
NG, TKG, TOPK = 8, 4, 8
GE = E // NG
SCALE = 2.5
NBS = (SI + P - 1) // P
NBE = E * I // P
assert NBE * P == E * I
NB = NBS + NBE
WB = 2 * KD * P + D
RING = 3
assert NBS == RING
LEAD = NH * NBS
TAIL = NB % RING
assert TAIL == 2
CW = 3 * E

GATE_BANK, UP_BANK, CW_BANK = (4, 7), 5, 6
SUM_PLACE = [(0, 0), (0, D), (2, 0), (2, D), (4, 0), (5, 0), (6, 0), (7, 0)]

LOGIT_BANK = (6, 1)
IN_SLOT = (2, 3, 0, 2, 3, 0, 3, 2)
QUARTER = TOK // 4
WARM0, WARM1, WARM2, WARM3 = 6, 8, 7, 6
MARK, NO_SCORE = -3.0e38, 3.0e38

OFF_NW = 0
OFF_CONV = OFF_NW + KD
OFF_CB = OFF_CONV + NQ * KC
OFF_XP = OFF_CB + NQ
OFF_DTW = OFF_XP + NQ * NX
OFF_DTB = OFF_DTW + NQ
OFF_AL = OFF_DTB + NQ
OFF_DP = OFF_AL + NQ * NS
OFF_RW = OFF_DP + NQ
NPAR = OFF_RW + KD * E


def build(nc, x, w_in, params, w_out, e_bias, w_moe, ident_d, sel_row_d, sel_c_d, sel_cw_d, out):
    with ExitStack() as ctx:
        def sb(name, shape, dt=F32):
            return ctx.enter_context(nc.sbuf_tensor(name, shape, dt))

        def sem(name):
            return ctx.enter_context(nc.semaphore(name))

        x_sb = sb("x_sb", [P, NT, D])
        x1 = sb("x1", [P, NT, D])
        wout = sb("wout", [P, NQ, D])
        par = sb("par", [P, NPAR])
        idn = sb("idn", [P, P])
        eb = sb("eb", [P, E])
        stats = sb("stats", [P, NT, 6])
        mv = sb("mv", [P, NT, 2])
        sd = sb("sd", [P, NT])
        rstd = sb("rstd", [P, NT])
        dv = sb("dv", [P, NT, 2])
        sdv = sb("sdv", [P, NT, 2])
        rdv = sb("rdv", [P, NT, 2])
        a_sb = sb("a_sb", [P, NQ * NS])
        xc = sb("xc", [P, NQ, TOK])
        sz = sb("sz", [P, NQ, TOK])
        ddiag = sb("ddiag", [P, NQ, P])
        selrow = sb("selrow", [NX, P])
        selc = sb("selc", [3 * 2 * NS, NS, P], BF16)

        with ExitStack() as early:
            def sbe(name, shape, dt=F32):
                return early.enter_context(nc.sbuf_tensor(name, shape, dt))

            xn = sbe("xn", [P, NT, D])
            cacc = sbe("cacc", [P, 2, TOK])
            win = sbe("win", [P, KD, 2 * DI])
            gap = 2 * NS // 4 * TOK - (NT * D + 2 * TOK + KD * 2 * DI)
            sbe("gap", [P, gap])
            xnh = sbe("xnh", [P, KD, TOK], F32R)
            xnl = sbe("xnl", [P, KD, TOK], F32R)
            winh = sbe("winh", [P, KD, 2 * DI], F32R)
            winl = sbe("winl", [P, KD, 2 * DI], F32R)

        with ExitStack() as scanning:
            def sbs(name, shape, dt=F32):
                return scanning.enter_context(nc.sbuf_tensor(name, shape, dt))

            bbc = sbs("bbc", [P, NS, TOK])
            xs = sbs("xs", [NX, TOK])
            xdt = sbs("xdt", [P, TOK])
            c3 = sbs("c3", [3 * 2 * NS, TOK], BF16)
            sp_abs = sbs("sp_abs", [P, TOK])
            sp_exp = sbs("sp_exp", [P, TOK])
            sp_w = sbs("sp_w", [P, TOK])
            sp_relu = sbs("sp_relu", [P, TOK])
            dt = sbs("dt", [P, 2, TOK])
            dtu = sbs("dtu", [P, 2, TOK])
            dbu = sbs("dbu", [P, 4, TOK])
            with ExitStack() as splitting:
                cmid = splitting.enter_context(nc.sbuf_tensor("cmid", [2 * NS, TOK], BF16))
                cres = splitting.enter_context(nc.sbuf_tensor("cres", [2 * NS, 2, TOK], F32))
            hs = sbs("hs", [P, 4, TOK])

        wraw = sb("wraw", [P, RING, WB])
        wh = sb("wh", [P, RING, WB], F32R)
        wl = sb("wl", [P, RING, WB], F32R)
        selcw = sb("selcw", [CW, NBE, P], BF16)
        xn2 = sb("xn2", [P, NT, D])
        x2 = sb("x2", [P, NT, D])
        xfh = sb("xfh", [P, KD, TOK], F32R)
        xfl = sb("xfl", [P, KD, TOK], F32R)
        cw3 = sb("cw3", [CW, TOK], BF16)
        scoresT = sb("scoresT", [E, TOK])
        rwh = sb("rwh", [P, KD, E], F32R)
        rwl = sb("rwl", [P, KD, E], F32R)
        cwb = sb("cwb", [P, 2, NT * E], BF16)
        cwp = sb("cwp", [P, NT, 3, E])
        rt = sb("rt", [P, 10, NT * E])
        sg = sb("sg", [P, 2, HALF])
        m1 = sb("m1", [P, 2, HALF])
        hbuf = sb("hbuf", [P, 2, HALF])
        hh = sb("hh", [P, 2, HALF], F32R)
        hl = sb("hl", [P, 2, HALF], F32R)
        sfc = rt[:, 9, :]
        ps = ctx.enter_context(nc.psum_tensor("ps", [P, 8, HALF], F32))

        def pair(k):
            return ps[:, 2 * k:2 * k + 2, :].rearrange("p a b -> p (a b)")

        b_scratch = nc.dram_tensor("b_scratch", [NS, TOK], F32, kind="Internal").ap()

        s_x = [sem(f"x_loaded{g}") for g in range(NH)]
        s_par = sem("params_loaded")
        s_id = sem("ident_loaded")
        s_win = [sem(f"w_in_loaded{g}") for g in range(2)]
        s_wout = sem("w_out_loaded")
        s_sel = sem("selectors_loaded")
        s_selcw = sem("cw_selector_loaded")
        s_bw = sem("b_rows_stored")
        s_bbc = sem("b_broadcast")
        s_out = sem("out_stored")

        dve_step = sem("dve_step")
        s_var = sem("variance_ready")
        s_sd = sem("deviation_ready")
        s_x1 = sem("x1_ready")
        s_xn = sem("xn_ready")
        s_tp = sem("transposed")
        s_xnh = sem("xn_high_ready")
        s_xnl = sem("xn_low_ready")
        s_winh = sem("w_in_high_ready")
        s_winl = sem("w_in_low_ready")
        s_inp = sem("in_proj_done")
        s_tap = sem("first_tap_ready")
        s_conv = sem("conv_ready")
        s_xc = sem("xc_ready")
        s_z = sem("silu_z_ready")
        s_xp = sem("x_proj_done")
        s_xs = sem("xs_ready")
        s_dtb = sem("dt_row_broadcast")
        s_xdt = sem("xdt_ready")
        s_c3 = sem("c_parts_ready")
        s_a = sem("a_ready")
        s_ea = sem("exp_a_log_ready")
        s_zero = sem("first_columns_zeroed")
        act_sp = sem("softplus_step")
        s_cor = sem("softplus_correction_ready")
        s_dt = sem("dt_ready")
        s_dtu = sem("dtu_ready")
        s_dd = sem("d_diagonal_ready")
        s_da = sem("decay_ready")
        s_dbu0 = sem("first_dbu_ready")
        s_dbu = sem("dbu_ready")
        s_scan = sem("scan_done")
        s_cb = sem("c_broadcast_done")
        s_hc = sem("hc_ready")
        s_y = sem("y_added")
        s_yz = sem("yz_ready")
        s_o = sem("out_proj_done")
        s_r = sem("residual_sum_ready")
        s_sd2 = sem("deviation2_ready")
        s_sd3 = sem("deviation3_ready")
        s_var2 = sem("variance2_ready")
        s_var3 = sem("variance3_ready")
        s_xf = sem("xf_ready")
        s_tp2 = sem("xf_transposed")
        s_lg = sem("logits_done")
        s_sc = sem("scores_ready")
        s_cmb = sem("combine_ready")
        s_cT = sem("combine_transposed")
        s_rwh = sem("router_weights_high_ready")
        s_rwl = sem("router_weights_low_ready")
        s_scT = sem("scores_transposed")
        s_xh = sem("xf_high_ready")
        s_xl = sem("xf_low_ready")
        s_cw3 = sem("combine_parts_ready")
        s_g = sem("gate_done")
        s_u = sem("up_done")
        s_c = sem("cw_broadcast_done")
        s_d = sem("down_done")
        s_sg = sem("silu_gate_ready")
        s_m1 = sem("gated_ready")
        s_h = sem("h_ready")
        s_hh = sem("h_high_ready")
        s_hl = sem("h_low_ready")
        s_wld = [sem(f"expert_weights_loaded{k}") for k in range(RING)]
        s_wh = sem("w_high_ready")
        s_wl = sem("w_low_ready")
        s_acc = sem("sums_copied")
        s_tp3 = sem("sums_transposed")
        s_var4 = sem("variance4_ready")
        s_sd4 = sem("deviation4_ready")
        s_fin = sem("final_ready")

        block = ctx.enter_context(nc.Block())

        @block.sync
        def _(sp):
            xt = x.rearrange("b s d -> (b s) d").rearrange("(t p) d -> p t d", p=P)

            def load_x(g):
                sp.dma_start(x_sb[:, g * TPH:(g + 1) * TPH, :], xt[:, g * TPH:(g + 1) * TPH, :]).then_inc(s_x[g], 16)

            def load_w_in(g):
                sp.dma_start(win[:, :, g * DI:(g + 1) * DI], w_in[:, :, g * DI:(g + 1) * DI]).then_inc(s_win[g], 16)

            load_x(0)
            sp.dma_start(idn[:], ident_d).then_inc(s_id, 16)
            sp.dma_start(par[:], params).then_inc(s_par, 16)
            load_x(1)
            load_w_in(0)
            load_w_in(1)
            sp.dma_start(selrow[:], sel_row_d).then_inc(s_sel, 16)
            sp.dma_start(selc[:], sel_c_d).then_inc(s_sel, 16)
            sp.dma_start(wout[:], w_out).then_inc(s_wout, 16)
            sp.dma_start(eb[:], e_bias.rearrange("(a e) -> a e", a=1).to_broadcast([P, E])).then_inc(s_wout, 16)
            sp.wait_ge(s_xs, 1)
            sp.dma_start(b_scratch, xs[0:NS, :]).then_inc(s_bw, 16)
            sp.wait_ge(s_bw, 16)
            sp.wait_ge(s_winl, 2)
            for k in range(4):
                if k:
                    sp.wait_ge(s_bbc, 16 * k)
                if k == 2:
                    sp.wait_ge(s_inp, 2 * NQ)
                src = b_scratch[4 * k:4 * k + 4, :].rearrange("(a n) t -> a n t", a=1).to_broadcast([P, 4, TOK])
                sp.dma_start(bbc[:, 4 * k:4 * k + 4, :], src).then_inc(s_bbc, 16)
            sp.wait_ge(s_dbu, NS * NQ - 1)
            sp.dma_start(selcw[:], sel_cw_d).then_inc(s_selcw, 16)
            for b in range(RING):
                sp.dma_start(wraw[:, b, :], w_moe[b]).then_inc(s_wld[b], 16)
            with sp.Fori(1, NB // RING) as m:
                for s in range(RING):
                    sp.wait_ge(s_wl, RING * m + (s - RING + 1))
                    sp.dma_start(wraw[:, s, :], w_moe[bass.ds(RING * m + s, 1), :, :].rearrange("a p w -> p (a w)")).then_inc(s_wld[s], 16)
            for b in range(NB - TAIL, NB):
                sp.wait_ge(s_wl, b - RING + 1)
                sp.dma_start(wraw[:, b % RING, :], w_moe[b]).then_inc(s_wld[b % RING], 16)
            ot = out.rearrange("b s d -> (b s) d").rearrange("(t p) d -> p t d", p=P)
            for g in range(NH):
                sp.wait_ge(s_fin, TPH * (g + 1))
                sp.dma_start(ot[:, g * TPH:(g + 1) * TPH, :], xn2[:, g * TPH:(g + 1) * TPH, :]).then_inc(s_out, 16)
            sp.wait_ge(s_out, 16 * NH)

        @block.tensor
        def _(pe):
            def keep_warm(n, bank, moving, cols):
                for _ in range(n):
                    nc.tensor.matmul(ps[:, bank, 0:cols], idn[:], moving, start=True, stop=True)

            pe.wait_ge(s_id, 16)
            keep_warm(WARM0, 7, idn[:], P)
            for g in range(NH):
                if g:
                    keep_warm(WARM1, 7, idn[:], P)
                for t in range(g * TPH, (g + 1) * TPH):
                    pe.wait_ge(s_xn, t + 1)
                    for k in range(KD):
                        mm = nc.tensor.transpose(ps[:, 2 * g + k, (t % TPH) * P:(t % TPH + 1) * P],
                                                 xn[:, t, k * P:(k + 1) * P], idn[:])
                mm.then_inc(s_tp, 1)
            keep_warm(WARM1, 7, idn[:], P)

            def in_proj(j):
                slot = IN_SLOT[j]
                rows = slice(j * P, (j + 1) * P)
                for h in range(NH):
                    if j == 0:
                        pe.wait_ge(s_xnl, KD * (h + 1))
                    cols = slice(h * HALF, (h + 1) * HALF)
                    for k in range(KD):
                        for n, (w, r) in enumerate(((winh, xnh), (winh, xnl), (winl, xnh))):
                            mm = nc.tensor.matmul(ps[:, 2 * slot + h, :], w[:, k, rows], r[:, k, cols],
                                                  start=(k == 0 and n == 0), stop=(k == KD - 1 and n == 2))
                mm.then_inc(s_inp, 1)

            def x_proj(j):
                pe.wait_ge(s_xc, j + 1)
                for h in range(NH):
                    mm = nc.tensor.matmul(ps[0:NX, 2 + h, :], par[:, OFF_XP + j * NX:OFF_XP + (j + 1) * NX],
                                          xc[:, j, h * HALF:(h + 1) * HALF], start=(j == 0), stop=(j == NQ - 1))
                mm.then_inc(s_xp, 1)

            pe.wait_ge(s_winl, 1)
            pe.wait_ge(s_par, 16)
            for j in range(NQ - 1):
                in_proj(j)
            pe.wait_ge(s_conv, 1)
            in_proj(3)
            pe.wait_ge(s_winl, 2)
            pe.wait_ge(s_conv, 2)
            in_proj(NQ)
            x_proj(0)
            x_proj(1)
            pe.wait_ge(s_conv, 3)
            in_proj(NQ + 1)
            x_proj(2)
            pe.wait_ge(s_z, 1)
            in_proj(NQ + 2)
            pe.wait_ge(s_conv, NQ)
            in_proj(NQ + 3)
            x_proj(NQ - 1)
            pe.wait_ge(s_xs, 1)
            pe.wait_ge(s_sel, 32)
            for h in range(NH):
                mm = nc.tensor.matmul(ps[:, 2 + h, :], selrow[:], xs[:, h * HALF:(h + 1) * HALF], start=True, stop=True)
            mm.then_inc(s_dtb, 1)

            def c_bcast(n, wait):
                pe.wait_ge(*wait)
                for h in range(NH):
                    lhs = selc[:, n, :] if not in_loop(n) else selc[:, bass.ds(n, 1), :].rearrange("p a b -> p (a b)")
                    mm = nc.tensor.matmul(ps[:, 4 + h, :], lhs, c3[:, h * HALF:(h + 1) * HALF], start=True, stop=True)
                mm.then_inc(s_cb, 1)

            def y_skip(q, piece):
                cols = bass.ds(piece * QUARTER, QUARTER) if in_loop(piece) else slice(piece * QUARTER, (piece + 1) * QUARTER)
                nc.tensor.matmul(pair(3)[:, cols], ddiag[:, q, :], xc[:, q, cols], start=False, stop=False,
                                 skip_group_check=True)

            def y_add(slot, wait, first=False, last=False):
                pe.wait_ge(*wait)
                for h in range(NH):
                    mm = nc.tensor.matmul(ps[:, 6 + h, :], idn[:], hs[:, slot, h * HALF:(h + 1) * HALF],
                                          start=first, stop=last, skip_group_check=True)
                mm.then_inc(s_y, 1)

            pe.wait_ge(s_z, NQ)
            for q in range(NQ):
                for k in range(4):
                    u = NS * q + k
                    c_bcast(k, (s_hc, u) if u else (s_c3, 1))
                    if u == 0:
                        keep_warm(WARM2, 7, xc[:, 0, 0:HALF], HALF)
                    if k == 1 and q:
                        pe.wait_ge(s_yz, q)
                    if u:
                        y_add((k - 1) % 4, (s_hc, u), first=(k == 1), last=(k == 0))
                    if u == 1:
                        pe.wait_ge(s_dd, 1)
                    if k == 3:
                        y_skip(q, 0)
                with pe.Fori(1, 4) as j:
                    for k in range(4):
                        c_bcast(4 * j + k, (s_hc, 4 * j + (NS * q + k)))
                        y_add((k - 1) % 4, (s_hc, 4 * j + (NS * q + k)))
                        if k == 2:
                            y_skip(q, j)

            def out_proj(t, blocks):
                for q in blocks:
                    mm = nc.tensor.matmul(ps[:, t, 0:D], sz[:, q, t * P:(t + 1) * P], wout[:, q, :],
                                          start=(q == 0), stop=(q == NQ - 1))
                return mm

            def y_add_half(h):
                pe.wait_ge(s_hc, NS * NQ + h)
                nc.tensor.matmul(ps[:, 6 + h, :], idn[:], hs[:, 3, h * HALF:(h + 1) * HALF], start=False, stop=True,
                                 skip_group_check=True).then_inc(s_y, 1)

            pe.wait_ge(s_wout, 32)
            y_add_half(0)
            pe.wait_ge(s_scan, NS * NQ)
            out_proj(0, range(NQ - 1))
            pe.wait_ge(s_yz, NQ)
            out_proj(0, [NQ - 1]).then_inc(s_o, 1)
            for t in range(1, TPH):
                out_proj(t, range(NQ)).then_inc(s_o, 1)
            y_add_half(1)
            out_proj(TPH, range(NQ - 1))
            pe.wait_ge(s_yz, NQ + 1)
            out_proj(TPH, [NQ - 1]).then_inc(s_o, 1)
            for t in range(TPH + 1, NT):
                out_proj(t, range(NQ)).then_inc(s_o, 1)

            def transpose_xf(g):
                for t in range(g * TPH, (g + 1) * TPH):
                    pe.wait_ge(s_xf, t + 1)
                    for k in range(KD):
                        mm = nc.tensor.transpose(ps[:, 2 * k + g, (t % TPH) * P:(t % TPH + 1) * P],
                                                 xn2[:, t, k * P:(k + 1) * P], idn[:])
                mm.then_inc(s_tp2, 1)

            def logits(h):
                pe.wait_ge(s_xl, KD * (h + 1))
                pe.wait_ge(s_rwl, 1)
                cols = slice(h * HALF, (h + 1) * HALF)
                for k in range(KD):
                    for n, (w, r) in enumerate(((rwh, xfh), (rwh, xfl), (rwl, xfh))):
                        mm = nc.tensor.matmul(ps[0:E, LOGIT_BANK[h], :], w[:, k, :], r[:, k, cols],
                                              start=(k == 0 and n == 0), stop=(k == KD - 1 and n == 2))
                mm.then_inc(s_lg, 1)

            def transpose_scores():
                pe.wait_ge(s_sc, NH)
                for t in range(NT):
                    mm = nc.tensor.transpose(ps[:, CW_BANK, t * E:(t + 1) * E], scoresT[:, t * P:(t + 1) * P],
                                             idn[0:E, 0:E])
                mm.then_inc(s_scT, 1)

            def transpose_combine(h):
                pe.wait_ge(s_cmb, 1)
                if h:
                    pe.wait_ge(s_cw3, h)
                for t in range(h * TPH, (h + 1) * TPH):
                    mm = nc.tensor.transpose(ps[0:CW, CW_BANK, (t % TPH) * P:(t % TPH + 1) * P],
                                             cwp[:, t, :, :].rearrange("p a e -> p (a e)"), idn[:])
                mm.then_inc(s_cT, 1)

            def three(dst, w_cols, rhs_h, rhs_l, slot, start, stop):
                for n, (w, r) in enumerate(((wh, rhs_h), (wh, rhs_l), (wl, rhs_h))):
                    mm = nc.tensor.matmul(dst, w[:, slot, w_cols], r, start=(start and n == 0), stop=(stop and n == 2),
                                          skip_group_check=True)
                return mm

            def gate_up(half, par2, slot, b, step, first):
                cols = slice(half * HALF, (half + 1) * HALF)
                pe.wait_ge(s_wl, b + 1)
                if not first:
                    pe.wait_ge(s_sg, step - 1)
                for k in range(KD):
                    mm = three(ps[:, GATE_BANK[par2], :], slice(k * P, (k + 1) * P), xfh[:, k, cols], xfl[:, k, cols],
                               slot, k == 0, k == KD - 1)
                mm.then_inc(s_g, 1)
                if not (first and step == 0):
                    pe.wait_ge(s_h, step)
                for k in range(KD):
                    mm = three(ps[:, UP_BANK, :], slice((KD + k) * P, (KD + k + 1) * P), xfh[:, k, cols],
                               xfl[:, k, cols], slot, k == 0, k == KD - 1)
                mm.then_inc(s_u, 1)

            def weigh(half, b):
                lhs = selcw[:, bass.ds(b - NBS, 1), :].rearrange("p a b -> p (a b)") if in_loop(b) else selcw[:, b - NBS, :]
                nc.tensor.matmul(ps[:, CW_BANK, :], lhs, cw3[:, half * HALF:(half + 1) * HALF],
                                 start=True, stop=True).then_inc(s_c, 1)

            def down(half, par2, slot, steps, first, last):
                pe.wait_ge(s_hl, steps)
                for dblk in range(KD):
                    mm = three(ps[:, 2 * dblk + half, :], slice(2 * KD * P + dblk * P, 2 * KD * P + (dblk + 1) * P),
                               hh[:, par2, :], hl[:, par2, :], slot, first, last)
                mm.then_inc(s_d, 1)

            def shared_down(i):
                down(i // NBS, i % 2, i % NBS, i + 1, i % NBS == 0, False)

            transpose_xf(0)
            keep_warm(WARM3, 1, idn[:], P)
            pe.wait_ge(s_xl, KD)
            for i in range(LEAD):
                if i == NBS:
                    logits(1)
                    shared_down(i - 1)
                gate_up(i // NBS, i % 2, i % NBS, i % NBS, i, i < 2)
                if i == 0:
                    logits(0)
                if i == NBS - 1:
                    transpose_xf(1)
                if i == NBS:
                    transpose_scores()
                if i and i != NBS:
                    shared_down(i - 1)
            gate_up(0, 0, 0, NBS, LEAD, False)
            for h in range(NH):
                transpose_combine(h)
            pe.wait_ge(s_cw3, NH)
            pe.wait_ge(s_selcw, 16)
            with pe.Fori(1, NB // RING) as m:
                for i in range(2 * RING):
                    prev, nxt = (i - 1) % (2 * RING), i + 1
                    weigh(i % 2, RING * m + i // 2)
                    down(prev % 2, prev % 2, prev // 2, 2 * RING * m + i, False, False)
                    gate_up(nxt % 2, nxt % 2, nxt // 2 % RING, RING * m + nxt // 2, 2 * RING * m + nxt, False)

            def transpose_sums(h):
                pe.wait_ge(s_acc, KD * (h + 1))
                for t in range(h * TPH, (h + 1) * TPH):
                    bank, col = SUM_PLACE[t]
                    for k in range(KD):
                        mm = nc.tensor.transpose(ps[:, bank, col + k * P:col + (k + 1) * P],
                                                 xc[:, k, t * P:(t + 1) * P], idn[:])
                    mm.then_inc(s_tp3, 1)

            first_step = 2 * (NB - TAIL)
            for i in range(2 * TAIL):
                b = NB - TAIL + i % TAIL
                if i:
                    gate_up(i // TAIL, i % 2, b % RING, b, first_step + i, False)
                weigh(i // TAIL, b)
                if i == 0:
                    down(1, 1, (b - 1) % RING, first_step, False, False)
                else:
                    down((i - 1) // TAIL, (i - 1) % 2, (NB - TAIL + (i - 1) % TAIL) % RING, first_step + i, False,
                         (i - 1) % TAIL == TAIL - 1)
            transpose_sums(0)
            down(1, 1, (NB - 1) % RING, 2 * NB, False, True)
            transpose_sums(1)

        @block.scalar
        def _(act):
            def deviations_x(g):
                ts = slice(g * TPH, (g + 1) * TPH)
                act.wait_ge(s_var, g + 1)
                nc.scalar.activation(sdv[:, ts, :], dv[:, ts, :], ACT.Sqrt).then_inc(s_sd, 1)

            def w_in_high(g):
                act.wait_ge(s_win[g], 16)
                nc.scalar.copy(winh[:, :, g * DI:(g + 1) * DI], win[:, :, g * DI:(g + 1) * DI]).then_inc(s_winh, 1)

            def xn_high(g):
                act.wait_ge(s_tp, g + 1)
                for k in range(KD):
                    nc.scalar.activation(xnh[:, k, g * HALF:(g + 1) * HALF], ps[:, 2 * g + k, :], ACT.Copy,
                                         scale=par[:, OFF_NW + k:OFF_NW + k + 1]).then_inc(s_xnh, 1)

            deviations_x(0)
            w_in_high(0)
            act.wait_ge(s_par, 16)
            xn_high(0)
            deviations_x(1)
            xn_high(1)
            w_in_high(1)

            def first_tap(j):
                slot = IN_SLOT[j]
                act.wait_ge(s_inp, j + 1)
                if j >= 2:
                    act.wait_ge(s_xc, j - 1)
                nc.scalar.activation(cacc[:, j % 2, :], pair(slot), ACT.Identity,
                                     scale=par[:, OFF_CONV + j * KC + KC - 1:OFF_CONV + j * KC + KC],
                                     bias=par[:, OFF_CB + j:OFF_CB + j + 1]).then_inc(s_tap, 1)

            def silu_xc(j):
                act.wait_ge(s_conv, j + 1)
                nc.scalar.activation(xc[:, j, :], cacc[:, j % 2, :], ACT.Silu).then_inc(s_xc, 1)

            def silu_z(j):
                act.wait_ge(s_inp, NQ + j + 1)
                nc.scalar.activation(sz[:, j, :], pair(IN_SLOT[NQ + j]), ACT.Silu).then_inc(s_z, 1)

            def softplus(q, steps=range(5)):
                sc, bi = par[:, OFF_DTW + q:OFF_DTW + q + 1], par[:, OFF_DTB + q:OFF_DTB + q + 1]
                n = 5 * q
                row = xdt[:] if q else pair(1)
                if 0 in steps:
                    if q:
                        act.wait_ge(s_dt, q)
                    nc.scalar.activation(sp_abs[:], row, ACT.Abs, scale=sc, bias=bi).then_inc(act_sp, 1)
                if 1 in steps:
                    act.wait_ge(act_sp, n + 1)
                    nc.scalar.activation(sp_exp[:], sp_abs[:], ACT.Exp, scale=-1.0).then_inc(act_sp, 1)
                if 2 in steps:
                    act.wait_ge(act_sp, n + 2)
                    nc.scalar.activation(sp_w[:], sp_exp[:], ACT.Identity, bias=1.0).then_inc(act_sp, 1)
                if 3 in steps:
                    nc.scalar.activation(sp_relu[:], row, ACT.Relu, scale=sc, bias=bi).then_inc(act_sp, 1)
                if 4 in steps:
                    act.wait_ge(act_sp, n + 3)
                    nc.scalar.activation(sp_abs[:], sp_w[:], ACT.Ln).then_inc(act_sp, 1)

            first_tap(0)
            first_tap(1)
            silu_xc(0)
            first_tap(2)
            silu_xc(1)
            first_tap(3)
            silu_z(0)
            silu_xc(2)
            silu_z(1)
            silu_xc(3)
            silu_z(2)
            silu_z(3)
            act.wait_ge(s_xp, NQ)
            nc.scalar.copy(xs[:], ps[0:NX, 2:4, :].rearrange("p a b -> p (a b)")).then_inc(s_xs, 1)
            nc.scalar.preload_act_table_set("natural_log_exp_and_others")
            nc.scalar.activation(a_sb[:], par[:, OFF_AL:OFF_AL + NQ * NS], ACT.Exp).then_inc(s_ea, 1)
            act.wait_ge(s_dtb, 1)
            softplus(0)
            nc.scalar.copy(xdt[:], pair(1)).then_inc(s_xdt, 1)

            def decay(q, n, slot, wait):
                act.wait_ge(*wait)
                dst = pair(slot).rearrange("p (b s) -> p b s", b=BATCH)[:, :, 1:SEQ]
                src = dt[:, q % 2, :].rearrange("p (b s) -> p b s", b=BATCH)[:, :, 1:SEQ]
                sc = a_sb[:, bass.ds(n + NS * q, 1)] if in_loop(n) else a_sb[:, NS * q + n:NS * q + n + 1]
                nc.scalar.activation(dst, src, ACT.Exp, scale=sc).then_inc(s_da, 1)

            act.wait_ge(s_zero, 1)
            act.wait_ge(s_a, 1)
            act.wait_ge(s_xdt, 1)
            for q in range(NQ):
                act.wait_ge(s_dt, q + 1)
                for k in range(4):
                    u = NS * q + k
                    decay(q, k, k % 2, (s_scan, u - 1) if u >= 2 else (s_zero, 1))
                    if k and q + 1 < NQ:
                        softplus(q + 1, ((), (0,), (1, 2), (3, 4))[k])
                with act.Fori(1, 4) as j:
                    for k in range(4):
                        decay(q, 4 * j + k, k % 2, (s_scan, 4 * j + (NS * q + k - 1)))

            def w_high(slot, wait_load, wait_down):
                act.wait_ge(s_wld[slot], wait_load)
                if wait_down is not None:
                    act.wait_ge(s_d, wait_down)
                nc.scalar.copy(wh[:, slot, :], wraw[:, slot, :]).then_inc(s_wh, 1)

            def deviation(g, s_v, s_dev):
                ts = slice(g * TPH, (g + 1) * TPH)
                act.wait_ge(s_v, g + 1)
                nc.scalar.activation(sd[:, ts], mv[:, ts, 1], ACT.Sqrt).then_inc(s_dev, 1)

            def x_high(g):
                act.wait_ge(s_tp2, g + 1)
                for k in range(KD):
                    nc.scalar.copy(xfh[:, k, g * HALF:(g + 1) * HALF], ps[:, 2 * k + g, :]).then_inc(s_xh, 1)

            def silu_gate(par2, step, first=False):
                act.wait_ge(s_g, step + 1)
                if not first:
                    act.wait_ge(s_h, step - 1)
                nc.scalar.activation(sg[:, par2, :], ps[:, GATE_BANK[par2], :], ACT.Silu).then_inc(s_sg, 1)

            def h_high(par2, step, first=False):
                act.wait_ge(s_h, step + 1)
                if not first:
                    act.wait_ge(s_d, step - 1)
                nc.scalar.copy(hh[:, par2, :], hbuf[:, par2, :]).then_inc(s_hh, 1)

            for b in range(NBS):
                w_high(b, 16, None)
            nc.scalar.copy(rwh[:], par[:, OFF_RW:OFF_RW + KD * E].rearrange("p (k e) -> p k e", k=KD)).then_inc(s_rwh, 1)
            deviation(0, s_var2, s_sd2)
            deviation(0, s_var3, s_sd3)
            x_high(0)
            deviation(1, s_var2, s_sd2)
            for i in range(LEAD):
                if i == 1:
                    deviation(1, s_var3, s_sd3)
                silu_gate(i % 2, i, i < 2)
                if i == LEAD - 1:
                    w_high(0, 32, NBS + 1)
                if i == NBS - 1:
                    x_high(1)
                h_high(i % 2, i, i < 2)
                if i == NBS - 1:
                    for h in range(NH):
                        act.wait_ge(s_lg, h + 1)
                        nc.scalar.activation(scoresT[:, h * HALF:(h + 1) * HALF], ps[0:E, LOGIT_BANK[h], :],
                                             ACT.Sigmoid).then_inc(s_sc, 1)
            for h in range(NH):
                act.wait_ge(s_cT, h + 1)
                nc.scalar.copy(cw3[:, h * HALF:(h + 1) * HALF], ps[0:CW, CW_BANK, :]).then_inc(s_cw3, 1)
            with act.Fori(1, NB // RING) as m:
                for s in range(RING):
                    silu_gate(0, 2 * RING * m + 2 * s)
                    h_high(0, 2 * RING * m + 2 * s)
                    if s + 1 < RING:
                        w_high(s + 1, 16 * m + 16, 2 * RING * m + (2 * (s + 1) - 3))
                    else:
                        w_high(0, 16 * m + 32, 2 * RING * m + (2 * RING - 3))
                    silu_gate(1, 2 * RING * m + (2 * s + 1))
                    h_high(1, 2 * RING * m + (2 * s + 1))
            w_high((NB - 1) % RING, 16 * ((NB - 1) // RING + 1), 2 * (NB - 1) - 3)
            for i in range(2 * TAIL):
                silu_gate(i % 2, 2 * (NB - TAIL) + i)
                h_high(i % 2, 2 * (NB - TAIL) + i)
                if i == TAIL:
                    act.wait_ge(s_d, 2 * NB - TAIL)
                    for k in range(KD):
                        nc.scalar.copy(xc[:, k, 0:HALF], ps[:, 2 * k, :]).then_inc(s_acc, 1)
            deviation(0, s_var4, s_sd4)
            act.wait_ge(s_d, 2 * NB)
            for k in range(KD):
                nc.scalar.copy(xc[:, k, HALF:TOK], ps[:, 2 * k + 1, :]).then_inc(s_acc, 1)
            deviation(1, s_var4, s_sd4)

        @block.gpsimd
        def _(pool):
            for g in range(2):
                rows = slice(g * DI, (g + 1) * DI)
                pool.wait_ge(s_winh, g + 1)
                nc.gpsimd.tensor_tensor(winl[:, :, rows], win[:, :, rows], winh[:, :, rows].bitcast(F32),
                                        ALU.subtract).then_inc(s_winl, 1)
            for t in range(NT):
                pool.wait_ge(s_xn, t + 1)
                nc.gpsimd.tensor_scalar(x1[:, t, :], x_sb[:, t, :], mv[:, t, 0:1], rdv[:, t, 0:1], ALU.subtract,
                                        ALU.mult).then_inc(s_x1, 1)

            def make_dtu(q):
                pool.wait_ge(s_dt, q + 1)
                if q >= 2:
                    pool.wait_ge(s_dbu, NS * (q - 1) - 1)
                nc.gpsimd.tensor_tensor(dtu[:, q % 2, :], dt[:, q % 2, :], xc[:, q, :], ALU.mult).then_inc(s_dtu, 1)

            def dbu_unit(q, n, slot, wait):
                if wait is not None:
                    pool.wait_ge(*wait)
                src = bbc[:, bass.ds(n, 1), :].rearrange("p a b -> p (a b)") if in_loop(n) else bbc[:, n, :]
                nc.gpsimd.tensor_tensor(dbu[:, slot, :], dtu[:, q % 2, :], src, ALU.mult).then_inc(s_dbu, 1)

            for q in range(NQ):
                pool.wait_ge(s_dtu, q + 1)
                if q == 0:
                    pool.wait_ge(s_bbc, 16)
                for k in range(q == 0, 4):
                    u = NS * q + k
                    dbu_unit(q, k, k, (s_scan, u - 3) if u >= 4 else None)
                with pool.Fori(1, 4) as j:
                    if q == 0:
                        pool.wait_ge(s_bbc, 16 * j + 16)
                    for k in range(4):
                        dbu_unit(q, 4 * j + k, k, (s_scan, 4 * j + (NS * q + k - 3)))
                if q + 1 < NQ:
                    make_dtu(q + 1)

            def w_low_pool(slot, b):
                pool.wait_ge(s_wh, b + 1)
                nc.gpsimd.tensor_tensor(wl[:, slot, :], wraw[:, slot, :], wh[:, slot, :].bitcast(F32),
                                        ALU.subtract).then_inc(s_wl, 1)

            for b in range(NBS):
                w_low_pool(b, b)
            pool.wait_ge(s_rwh, 1)
            nc.gpsimd.tensor_tensor(rwl[:], par[:, OFF_RW:OFF_RW + KD * E].rearrange("p (k e) -> p k e", k=KD),
                                    rwh[:].bitcast(F32), ALU.subtract).then_inc(s_rwl, 1)

            def low(par2, step, first):
                pool.wait_ge(s_hh, step + 1)
                if not first:
                    pool.wait_ge(s_d, step - 1)
                nc.gpsimd.tensor_tensor(hl[:, par2, :], hbuf[:, par2, :], hh[:, par2, :].bitcast(F32),
                                        ALU.subtract).then_inc(s_hl, 1)

            for i in range(LEAD):
                if i == LEAD - 1:
                    w_low_pool(0, NBS)
                low(i % 2, i, i < 2)
            with pool.Fori(1, NB // RING) as m:
                for i in range(2 * RING):
                    low(i % 2, 2 * RING * m + i, False)
            for i in range(2 * (NB - TAIL), 2 * NB):
                low(i % 2, i, False)

        @block.vector
        def _(dve):
            count = [0]

            def after(ins):
                count[0] += 1
                ins.then_inc(dve_step, 1)
                dve.wait_ge(dve_step, count[0])

            def moments(src, g, s_ready):
                for t in range(g * TPH, (g + 1) * TPH):
                    last = nc.vector.bn_stats(stats[:, t, :], src(t))
                after(last)
                for t in range(g * TPH, (g + 1) * TPH):
                    last = nc.vector.bn_aggr(mv[:, t, :], stats[:, t, :])
                after(last)
                ts = slice(g * TPH, (g + 1) * TPH)
                nc.vector.tensor_scalar(mv[:, ts, 1], mv[:, ts, 1], EPS, None, ALU.add).then_inc(s_ready, 1)

            def inverse(g, s_dev):
                ts = slice(g * TPH, (g + 1) * TPH)
                dve.wait_ge(s_dev, g + 1)
                after(nc.vector.reciprocal(rstd[:, ts], sd[:, ts]))

            def normed(dst, src, t):
                return nc.vector.tensor_scalar(dst, src, mv[:, t, 0:1], rstd[:, t:t + 1], ALU.subtract, ALU.mult)

            def both_norms(g):
                ts = slice(g * TPH, (g + 1) * TPH)
                dve.wait_ge(s_x[g], 16)
                for t in range(g * TPH, (g + 1) * TPH):
                    last = nc.vector.bn_stats(stats[:, t, :], x_sb[:, t, :])
                after(last)
                for t in range(g * TPH, (g + 1) * TPH):
                    last = nc.vector.bn_aggr(mv[:, t, :], stats[:, t, :])
                after(last)
                after(nc.vector.tensor_scalar(dv[:, ts, 0], mv[:, ts, 1], EPS, None, ALU.add))
                nc.vector.scalar_tensor_tensor(out=dv[:, ts, 1], in0=dv[:, ts, 0], scalar=EPS, in1=mv[:, ts, 1],
                                               op0=ALU.mult, op1=ALU.add).then_inc(s_var, 1)
                dve.wait_ge(s_sd, g + 1)
                after(nc.vector.reciprocal(rdv[:, ts, :], sdv[:, ts, :]))
                for t in range(g * TPH, (g + 1) * TPH):
                    nc.vector.tensor_scalar(xn[:, t, :], x_sb[:, t, :], mv[:, t, 0:1], rdv[:, t, 1:2], ALU.subtract,
                                            ALU.mult).then_inc(s_xn, 1)

            def xn_low(g):
                dve.wait_ge(s_par, 16)
                for k in range(KD):
                    cols, nw = slice(g * HALF, (g + 1) * HALF), par[:, OFF_NW + k:OFF_NW + k + 1]
                    dve.wait_ge(s_xnh, KD * g + k + 1)
                    nc.vector.scalar_tensor_tensor(out=xnl[:, k, cols], in0=ps[:, 2 * g + k, :], scalar=nw,
                                                   in1=xnh[:, k, cols].bitcast(F32), op0=ALU.mult,
                                                   op1=ALU.subtract).then_inc(s_xnl, 1)

            both_norms(0)
            both_norms(1)
            xn_low(0)
            xn_low(1)
            for q in range(NQ):
                last = nc.vector.tensor_scalar(ddiag[:, q, :], idn[:], par[:, OFF_DP + q:OFF_DP + q + 1], None, ALU.mult)
            last.then_inc(s_dd, 1)
            for j in range(NQ):
                slot = IN_SLOT[j]
                xi = pair(slot).rearrange("p (b s) -> p b s", b=BATCH)
                acc = cacc[:, j % 2, :].rearrange("p (b s) -> p b s", b=BATCH)
                dve.wait_ge(s_tap, j + 1)
                for shift in range(1, KC):
                    w = par[:, OFF_CONV + j * KC + KC - 1 - shift:OFF_CONV + j * KC + KC - shift]
                    ins = nc.vector.scalar_tensor_tensor(out=acc[:, :, shift:SEQ], in0=xi[:, :, 0:SEQ - shift], scalar=w,
                                                         in1=acc[:, :, shift:SEQ], op0=ALU.mult, op1=ALU.add)
                    if shift < KC - 1:
                        after(ins)
                    else:
                        ins.then_inc(s_conv, 1)

            dve.wait_ge(s_ea, 1)
            nc.vector.tensor_scalar(a_sb[:], a_sb[:], -1.0, None, ALU.mult).then_inc(s_a, 1)
            after(nc.vector.tensor_copy(c3[0:2 * NS, :], xs[0:2 * NS, :]))
            after(nc.vector.tensor_tensor(cres[:, 0, :], xs[0:2 * NS, :], c3[0:2 * NS, :], ALU.subtract))
            after(nc.vector.tensor_copy(cmid[:], cres[:, 0, :]))
            after(nc.vector.tensor_tensor(cres[:, 1, :], cres[:, 0, :], cmid[:], ALU.subtract))
            nc.vector.tensor_copy(c3[2 * NS:4 * NS, :], cmid[:])
            nc.vector.tensor_copy(c3[4 * NS:6 * NS, :], cres[:, 1, :]).then_inc(s_c3, 1)

            def correction(q):
                dve.wait_ge(act_sp, 5 * q + 3)
                nc.vector.scalar_tensor_tensor(out=sp_exp[:], in0=sp_w[:], scalar=1.0, in1=sp_exp[:],
                                               op0=ALU.subtract, op1=ALU.subtract).then_inc(s_cor, 1)

            def corrected(q):
                dve.wait_ge(act_sp, 5 * q + 4)
                dve.wait_ge(s_cor, 2 * q + 1)
                nc.vector.tensor_tensor(sp_relu[:], sp_relu[:], sp_exp[:], ALU.subtract).then_inc(s_cor, 1)

            def make_dt(q):
                dve.wait_ge(act_sp, 5 * q + 5)
                dve.wait_ge(s_cor, 2 * q + 2)
                if q >= 2:
                    dve.wait_ge(s_da, NS * (q - 1))
                    dve.wait_ge(s_dtu, q - 1)
                nc.vector.tensor_tensor(dt[:, q % 2, :], sp_relu[:], sp_abs[:], ALU.add).then_inc(s_dt, 1)

            def scan(slot2, slot4, u, wait_y):
                dve.wait_ge(s_da, u + 1)
                first = not wait_y and u == 0
                dve.wait_ge(s_dbu0 if first else s_dbu, 1 if first else u)
                if wait_y:
                    dve.wait_ge(s_y, u - 3)
                nc.vector.tensor_tensor_scan(hs[:, slot4, :], pair(slot2), dbu[:, slot4, :], 0.0,
                                             ALU.mult, ALU.add).then_inc(s_scan, 1)

            def times_c(slot4, u1):
                dve.wait_ge(s_scan, u1)
                dve.wait_ge(s_cb, u1)
                nc.vector.tensor_tensor(hs[:, slot4, :], hs[:, slot4, :], pair(2), ALU.mult).then_inc(s_hc, 1)

            def gate_y(q):
                dve.wait_ge(s_y, NS * (q + 1))
                nc.vector.tensor_tensor(sz[:, q, :], pair(3), sz[:, q, :], ALU.mult).then_inc(s_yz, 1)

            correction(0)
            corrected(0)
            make_dt(0)
            dve.wait_ge(s_dt, 1)
            nc.vector.tensor_tensor(dtu[:, 0, :], dt[:, 0, :], xc[:, 0, :], ALU.mult).then_inc(s_dtu, 1)
            dve.wait_ge(s_z, 2)
            dve.wait_ge(s_xdt, 1)
            nc.vector.memset(ps[:, 0:4, :].rearrange("p a (b s) -> p (a b) s", s=SEQ)[:, :, 0:1], 0.0).then_inc(s_zero, 1)
            dve.wait_ge(s_bbc, 16)
            dve.wait_ge(s_dtu, 1)
            nc.vector.tensor_tensor(dbu[:, 0, :], dtu[:, 0, :], bbc[:, 0, :], ALU.mult).then_inc(s_dbu0, 1)
            dve.wait_ge(s_c3, 1)
            for q in range(NQ):
                for k in range(4):
                    u = NS * q + k
                    scan(k % 2, k, u, u >= 4)
                    if u:
                        times_c((k - 1) % 4, u)
                    if k == 1 and q:
                        gate_y(q - 1)
                for k in range(4):
                    if q + 1 < NQ and k < 3:
                        (correction, corrected, make_dt)[k](q + 1)
                    scan(k % 2, k, NS * q + 4 + k, True)
                    times_c((k - 1) % 4, NS * q + 4 + k)
                with dve.Fori(2, 4) as j:
                    for k in range(4):
                        scan(k % 2, k, 4 * j + (NS * q + k), True)
                        times_c((k - 1) % 4, 4 * j + (NS * q + k))
            for h in range(NH):
                cols = slice(h * HALF, (h + 1) * HALF)
                dve.wait_ge(s_scan, NS * NQ)
                dve.wait_ge(s_cb, NS * NQ)
                nc.vector.tensor_tensor(hs[:, 3, cols], hs[:, 3, cols], ps[:, 4 + h, :], ALU.mult).then_inc(s_hc, 1)

            def gate_last(h):
                cols = slice(h * HALF, (h + 1) * HALF)
                dve.wait_ge(s_y, NS * NQ + h)
                nc.vector.tensor_tensor(sz[:, NQ - 1, cols], ps[:, 6 + h, :], sz[:, NQ - 1, cols],
                                        ALU.mult).then_inc(s_yz, 1)

            gate_last(0)

            def resid(t):
                dve.wait_ge(s_o, t + 1)
                return nc.vector.tensor_tensor(x1[:, t, :], ps[:, t, 0:D], x1[:, t, :], ALU.add)

            def aggregate(g, s_ready):
                for t in range(g * TPH, (g + 1) * TPH):
                    last = nc.vector.bn_aggr(mv[:, t, :], stats[:, t, :])
                after(last)
                ts = slice(g * TPH, (g + 1) * TPH)
                nc.vector.tensor_scalar(mv[:, ts, 1], mv[:, ts, 1], EPS, None, ALU.add).then_inc(s_ready, 1)

            def norm_sum(g):
                inverse(g, s_sd2)
                for t in range(g * TPH, (g + 1) * TPH):
                    last = normed(x1[:, t, :], x1[:, t, :], t)
                return last

            def norm_x2(g):
                inverse(g, s_sd3)
                for t in range(g * TPH, (g + 1) * TPH):
                    normed(xn2[:, t, :], x2[:, t, :], t).then_inc(s_xf, 1)

            def make_x2(g):
                for t in range(g * TPH, (g + 1) * TPH):
                    last = nc.vector.tensor_tensor(x2[:, t, :], x_sb[:, t, :], x1[:, t, :], ALU.add)
                return last

            def x_low(g):
                for k in range(KD):
                    cols = slice(g * HALF, (g + 1) * HALF)
                    dve.wait_ge(s_xh, KD * g + k + 1)
                    nc.vector.tensor_tensor(xfl[:, k, cols], ps[:, 2 * k + g, :], xfh[:, k, cols].bitcast(F32),
                                            ALU.subtract).then_inc(s_xl, 1)

            def w_low(slot, wait_high):
                dve.wait_ge(s_wh, wait_high)
                nc.vector.tensor_tensor(wl[:, slot, :], wraw[:, slot, :], wh[:, slot, :].bitcast(F32),
                                        ALU.subtract).then_inc(s_wl, 1)

            def shared_step(par2, step):
                dve.wait_ge(s_sg, step + 1)
                dve.wait_ge(s_u, step + 1)
                if step >= 2:
                    dve.wait_ge(s_hl, step - 1)
                nc.vector.tensor_tensor(hbuf[:, par2, :], ps[:, UP_BANK, :], sg[:, par2, :], ALU.mult).then_inc(s_h, 1)

            dve.wait_ge(s_x1, NT)
            for t in range(TPH):
                after(resid(t))
                last = nc.vector.bn_stats(stats[:, t, :], x1[:, t, :])
            after(last)
            aggregate(0, s_var2)
            gate_last(1)
            after(norm_sum(0))
            after(make_x2(0))
            moments(lambda t: x2[:, t, :], 0, s_var3)
            norm_x2(0)
            for t in range(TPH, NT):
                last = resid(t)
            x_low(0)
            after(last)
            moments(lambda t: x1[:, t, :], 1, s_var2)
            after(norm_sum(1))
            shared_step(0, 0)
            after(make_x2(1))
            moments(lambda t: x2[:, t, :], 1, s_var3)
            norm_x2(1)
            shared_step(1, 1)
            shared_step(0, 2)
            x_low(1)

            def r3(a):
                return a.rearrange("p (t e) -> p t e", t=NT)

            def r4(a):
                return a.rearrange("p (t g e) -> p t g e", t=NT, g=NG)

            scores = ps[:, CW_BANK, 0:NT * E]
            dve.wait_ge(s_wout, 32)
            dve.wait_ge(s_scT, 1)
            ebb = eb[:].rearrange("p (a e) -> p a e", a=1).to_broadcast([P, NT, E])
            after(nc.vector.tensor_tensor(r3(sfc), r3(scores), ebb, ALU.add))
            shared_step(1, 3)
            W = NT * NG

            def v(slot, part):
                return rt[:, slot, part * W:(part + 1) * W].rearrange("p (t g) -> p t g", t=NT)

            def pairs(part):
                return rt[:, 1, 2 * part * W:2 * (part + 1) * W].rearrange("p (t g e) -> p t g e", t=NT, g=NG)

            even, odd = r4(sfc)[:, :, :, 0:GE:2], r4(sfc)[:, :, :, 1:GE:2]
            nc.vector.tensor_tensor(pairs(0), even, odd, ALU.max)
            after(nc.vector.tensor_tensor(pairs(1), even, odd, ALU.min))
            nc.vector.tensor_tensor(v(2, 0), pairs(0)[:, :, :, 0], pairs(0)[:, :, :, 1], ALU.max)
            nc.vector.tensor_tensor(v(2, 1), pairs(0)[:, :, :, 0], pairs(0)[:, :, :, 1], ALU.min)
            after(nc.vector.tensor_tensor(v(2, 2), pairs(1)[:, :, :, 0], pairs(1)[:, :, :, 1], ALU.max))
            after(nc.vector.tensor_tensor(v(2, 3), v(2, 1), v(2, 2), ALU.max))
            after(nc.vector.tensor_tensor(v(3, 0), v(2, 0), v(2, 3), ALU.add))
            for t in range(NT):
                last = nc.vector.max(rt[:, 5, t * NG:(t + 1) * NG], v(3, 0)[:, t, :])
            after(last)
            after(nc.vector.memset(rt[:, 5, 0:NT * NG].rearrange("p (t g) -> p t g", t=NT)[:, :, TKG:NG], NO_SCORE))
            for t in range(NT):
                last = nc.vector.match_replace(out=v(3, 1)[:, t, :], in_to_replace=rt[:, 5, t * NG:(t + 1) * NG],
                                               in_values=v(3, 0)[:, t, :], imm_value=MARK)
            after(last)
            after(nc.vector.tensor_scalar(v(2, 0), v(3, 1), MARK, None, ALU.is_equal))
            gm = rt[:, 2, 0:W].rearrange("p (t g e) -> p t g e", t=NT, e=1).to_broadcast([P, NT, NG, GE])
            after(nc.vector.tensor_tensor(r4(rt[:, 4, :]), r4(sfc), gm, ALU.mult))
            after(nc.vector.tensor_scalar(rt[:, 4, :], rt[:, 4, :], 0.0, None, ALU.add))
            for t in range(NT):
                last = nc.vector.max(rt[:, 5, t * TOPK:(t + 1) * TOPK], rt[:, 4, t * E:(t + 1) * E])
            shared_step(0, 4)
            after(last)
            for t in range(NT):
                last = nc.vector.match_replace(out=rt[:, 6, t * E:(t + 1) * E],
                                               in_to_replace=rt[:, 5, t * TOPK:(t + 1) * TOPK],
                                               in_values=rt[:, 4, t * E:(t + 1) * E], imm_value=MARK)
            after(last)
            after(nc.vector.scalar_tensor_tensor(out=rt[:, 7, :], in0=rt[:, 6, :], scalar=MARK, in1=scores,
                                                 op0=ALU.is_equal, op1=ALU.mult))
            after(nc.vector.tensor_reduce(rt[:, 5, 0:NT], r3(rt[:, 7, :]), AX.X, ALU.add))
            after(nc.vector.tensor_scalar(rt[:, 5, 0:NT], rt[:, 5, 0:NT], 1e-20, None, ALU.add))
            after(nc.vector.reciprocal(rt[:, 5, NT:2 * NT], rt[:, 5, 0:NT]))
            inv = rt[:, 5, NT:2 * NT].rearrange("p (t e) -> p t e", e=1).to_broadcast([P, NT, E])
            after(nc.vector.scalar_tensor_tensor(out=r3(rt[:, 0, :]), in0=r3(rt[:, 7, :]), scalar=SCALE, in1=inv,
                                                 op0=ALU.mult, op1=ALU.mult))
            after(nc.vector.tensor_copy(cwb[:, 0, :], rt[:, 0, :]))
            after(nc.vector.tensor_tensor(rt[:, 1, :], rt[:, 0, :], cwb[:, 0, :], ALU.subtract))
            nc.vector.tensor_copy(cwp[:, :, 0, :], r3(cwb[:, 0, :]))
            after(nc.vector.tensor_copy(cwb[:, 1, :], rt[:, 1, :]))
            nc.vector.tensor_copy(cwp[:, :, 1, :], r3(cwb[:, 1, :]))
            nc.vector.tensor_tensor(cwp[:, :, 2, :], r3(rt[:, 1, :]), r3(cwb[:, 1, :]), ALU.subtract).then_inc(s_cmb, 1)
            shared_step(1, 5)

            def routed_step(par2, step):
                dve.wait_ge(s_sg, step + 1)
                dve.wait_ge(s_u, step + 1)
                dve.wait_ge(s_h, step - 1)
                nc.vector.tensor_tensor(m1[:, par2, :], ps[:, UP_BANK, :], sg[:, par2, :], ALU.mult).then_inc(s_m1, 1)
                dve.wait_ge(s_m1, step + (1 - LEAD))
                dve.wait_ge(s_c, step + (1 - LEAD))
                dve.wait_ge(s_hl, step - 1)
                nc.vector.tensor_tensor(hbuf[:, par2, :], ps[:, CW_BANK, :], m1[:, par2, :], ALU.mult).then_inc(s_h, 1)

            with dve.Fori(1, NB // RING) as m:
                for s in range(RING):
                    routed_step(0, 2 * RING * m + 2 * s)
                    w_low((s + 1) % RING, RING * m + (s + 2))
                    routed_step(1, 2 * RING * m + (2 * s + 1))
            w_low((NB - 1) % RING, NB)
            for i in range(2 * (NB - TAIL), 2 * NB):
                routed_step(i % 2, i)

            def sums(t):
                bank, col = SUM_PLACE[t]
                return ps[:, bank, col:col + D]

            for g in range(NH):
                dve.wait_ge(s_tp3, TPH * (g + 1))
                moments(sums, g, s_var4)
                inverse(g, s_sd4)
                for t in range(g * TPH, (g + 1) * TPH):
                    last = normed(x1[:, t, :], sums(t), t)
                after(last)
                for t in range(g * TPH, (g + 1) * TPH):
                    nc.vector.tensor_tensor(xn2[:, t, :], x2[:, t, :], x1[:, t, :], ALU.add).then_inc(s_fin, 1)


def in_loop(n):
    return not isinstance(n, int)


def kernel(**inputs):
    import concourse.bacc as bacc
    import ml_dtypes
    from concourse.bass_utils import run_bass_kernel_spmd as run

    def a(name):
        return np.asarray(inputs["L0_" + name])

    def rows(m, n):
        return m.reshape(n, P, -1).transpose(1, 0, 2)

    params = np.concatenate([
        rows(a("attn_norm_w"), KD).reshape(P, -1),
        rows(a("attn_conv_w").reshape(DI, KC), NQ).reshape(P, -1),
        rows(a("attn_conv_b"), NQ).reshape(P, -1),
        rows(a("attn_x_proj_w").T, NQ).reshape(P, -1),
        rows(a("attn_dt_w"), NQ).reshape(P, -1),
        rows(a("attn_dt_b"), NQ).reshape(P, -1),
        rows(a("attn_A_log"), NQ).reshape(P, -1),
        rows(a("attn_D_param"), NQ).reshape(P, -1),
        rows(a("ffn_router_weight").T, KD).reshape(P, -1),
    ], axis=1)
    pad = np.zeros((NB * P - E * I - SI, D), np.float32)

    def blocks(routed, shared):
        return np.concatenate([shared, pad, routed]).reshape(NB, P, D)

    def stationary(w):
        return w.reshape(NB, P, KD, P).transpose(0, 3, 2, 1).reshape(NB, P, KD * P)

    gate = stationary(blocks(a("ffn_Wg").reshape(E * I, D), a("ffn_sWg")))
    up = stationary(blocks(a("ffn_Wu").reshape(E * I, D), a("ffn_sWu")))
    down = blocks(a("ffn_Wd").transpose(0, 2, 1).reshape(E * I, D), a("ffn_sWd").T)
    sel_row = np.zeros((NX, P), np.float32)
    sel_row[NX - 1] = 1
    sel_c = np.zeros((3, 2 * NS, NS, P), ml_dtypes.bfloat16)
    for n in range(NS):
        sel_c[:, NS + n, n] = 1
    sel_cw = np.zeros((CW, NBE * P), ml_dtypes.bfloat16)
    for e in range(E):
        for part in range(3):
            sel_cw[part * E + e, e * I:(e + 1) * I] = 1
    arrays = {
        "x": a("attn_x"),
        "w_in": rows(a("attn_in_proj_w").T, KD),
        "params": params,
        "w_out": rows(a("attn_out_proj_w").T, NQ),
        "e_bias": a("ffn_e_bias"),
        "w_moe": np.concatenate([gate, up, down], axis=2),
        "ident": np.eye(P, dtype=np.float32),
        "sel_row": sel_row,
        "sel_c": sel_c.reshape(3 * 2 * NS, NS, P),
        "sel_cw": sel_cw.reshape(CW, NBE, P),
    }
    arrays = {n: np.ascontiguousarray(v) for n, v in arrays.items()}
    nc = bacc.Bacc("TRN2", target_bir_lowering=False, num_devices=1)
    aps = [nc.dram_tensor(n, v.shape, mybir.dt.from_np(v.dtype), kind="ExternalInput").ap() for n, v in arrays.items()]
    aps.append(nc.dram_tensor("out", (BATCH, SEQ, D), F32, kind="ExternalOutput").ap())
    build(nc, *aps)
    return run(nc, [arrays], core_ids=[0]).results[0]["out"]
```

```python
import math
from contextlib import ExitStack

import concourse.bass as bass
import numpy as np
from concourse import mybir

ALU = mybir.AluOpType
ACT = mybir.ActivationFunctionType
AX = mybir.AxisListType
F32 = mybir.dt.float32
F32R = mybir.dt.float32r
BF16 = mybir.dt.bfloat16

P = 128
BATCH, SEQ, D = 4, 256, 256
TOK = BATCH * SEQ
NT = TOK // P
HALF = 512
NH = TOK // HALF
TPH = NT // NH
KD = D // P
DI = 512
NQ = DI // P
NS = 16
KC = 4
NX = 2 * NS + 1
EPS = 1e-5
E, I, SI = 32, 176, 352
NG, TKG, TOPK = 8, 4, 8
GE = E // NG
SCALE = 2.5
NBS = (SI + P - 1) // P
NBE = E * I // P
assert NBE * P == E * I
NB = NBS + NBE
WB = 2 * KD * P + D
RING = 3
assert NBS == RING
LEAD = NH * NBS
TAIL = NB % RING
assert TAIL == 2
GROUP = math.gcd(I, P)
GPE, GPB = I // GROUP, P // GROUP

GATE_BANK, UP_BANK = (4, 7), (5, 6)
ROUTER_BANK = UP_BANK[1]
SUM_PLACE = [(0, 0), (0, D), (2, 0), (2, D), (4, 0), (5, 0), (6, 0), (7, 0)]

LOGIT_BANK = (ROUTER_BANK, 1)
IN_ORDER = (0, 1, 2, 4, 3, 5, 6, 7)
IN_SLOT = (2, 3, 0, 2, 1, 0, 3, 2)
QUARTER = TOK // 4
WARM_START, WARM_BETWEEN, WARM_IN_PROJ, WARM_SOFTPLUS, WARM_SCAN = 6, 8, 4, 5, 5
MARK, NO_SCORE = -3.0e38, 3.0e38

OFF_NW = 0
OFF_CONV = OFF_NW + KD
OFF_CB = OFF_CONV + NQ * KC
OFF_XP = OFF_CB + NQ
OFF_DTW = OFF_XP + NQ * NX
OFF_DTB = OFF_DTW + NQ
OFF_AL = OFF_DTB + NQ
OFF_DP = OFF_AL + NQ * NS
OFF_RW = OFF_DP + NQ
NPAR = OFF_RW + KD * E


def experts_of(block):
    lo, hi = block * P, (block + 1) * P
    return [(e, max(e * I, lo) - lo, min((e + 1) * I, hi) - lo) for e in range(lo // I, (hi - 1) // I + 1)]


def build(nc, x, w_in, params, w_out, e_bias, w_moe, ident_d, sel_row_d, sel_c_d, out):
    with ExitStack() as ctx:
        def sb(name, shape, dt=F32):
            return ctx.enter_context(nc.sbuf_tensor(name, shape, dt))

        def sem(name):
            return ctx.enter_context(nc.semaphore(name))

        x_sb = sb("x_sb", [P, NT, D])
        x1 = sb("x1", [P, NT, D])
        wout = sb("wout", [P, NQ, D])
        par = sb("par", [P, NPAR])
        idn = sb("idn", [P, P])
        eb = sb("eb", [P, E])
        stats = sb("stats", [P, NT, 6])
        mv = sb("mv", [P, NT, 2])
        sd = sb("sd", [P, NT])
        rstd = sb("rstd", [P, NT])
        nmr = sb("nmr", [P, NT])
        dv = sb("dv", [P, NT, 2])
        sdv = sb("sdv", [P, NT, 2])
        rdv = sb("rdv", [P, NT, 2])
        a_sb = sb("a_sb", [P, NQ * NS])
        xc = sb("xc", [P, NQ, TOK])
        sz = sb("sz", [P, NQ, TOK])
        ddiag = sb("ddiag", [P, NQ, P])
        selrow = sb("selrow", [NX, P])
        selc = sb("selc", [3 * 2 * NS, NS, P], BF16)

        with ExitStack() as early:
            def sbe(name, shape, dt=F32):
                return early.enter_context(nc.sbuf_tensor(name, shape, dt))

            xn = sbe("xn", [P, NT, D])
            cacc = sbe("cacc", [P, 2, TOK])
            win = sbe("win", [P, KD, 2 * DI])
            gap = 2 * NS // 4 * TOK - (NT * D + 2 * TOK + KD * 2 * DI)
            sbe("gap", [P, gap])
            xnh = sbe("xnh", [P, KD, TOK], F32R)
            xnl = sbe("xnl", [P, KD, TOK], F32R)
            winh = sbe("winh", [P, KD, 2 * DI], F32R)
            winl = sbe("winl", [P, KD, 2 * DI], F32R)

        with ExitStack() as scanning:
            def sbs(name, shape, dt=F32):
                return scanning.enter_context(nc.sbuf_tensor(name, shape, dt))

            bbc = sbs("bbc", [P, NS, TOK])
            xs = sbs("xs", [NX, TOK])
            xdt = sbs("xdt", [P, TOK])
            c3 = sbs("c3", [3 * 2 * NS, TOK], BF16)
            sp_abs = sbs("sp_abs", [P, TOK])
            sp_exp = sbs("sp_exp", [P, TOK])
            sp_w = sbs("sp_w", [P, TOK])
            sp_relu = sbs("sp_relu", [P, TOK])
            dt = sbs("dt", [P, 2, TOK])
            dtu = sbs("dtu", [P, 2, TOK])
            dbu = sbs("dbu", [P, 4, TOK])
            with ExitStack() as splitting:
                cmid = splitting.enter_context(nc.sbuf_tensor("cmid", [2 * NS, TOK], BF16))
                cres = splitting.enter_context(nc.sbuf_tensor("cres", [2 * NS, 2, TOK], F32))
            hs = sbs("hs", [P, 4, TOK])

        wraw = sb("wraw", [P, RING, WB])
        wh = sb("wh", [P, RING, WB], F32R)
        wl = sb("wl", [P, RING, WB], F32R)
        cwrow = sb("cwrow", [P, RING, TOK])
        xn2 = sb("xn2", [P, NT, D])
        x2 = sb("x2", [P, NT, D])
        xfh = sb("xfh", [P, KD, TOK], F32R)
        xfl = sb("xfl", [P, KD, TOK], F32R)
        cwT = sb("cwT", [P, NH, P])
        scoresT = sb("scoresT", [E, TOK])
        rwh = sb("rwh", [P, KD, E], F32R)
        rwl = sb("rwl", [P, KD, E], F32R)
        rt = sb("rt", [P, 10, NT * E])
        sg = sb("sg", [P, 2, HALF])
        m1 = sb("m1", [P, 2, HALF])
        hbuf = sb("hbuf", [P, 2, HALF])
        hh = sb("hh", [P, 2, HALF], F32R)
        hl = sb("hl", [P, 2, HALF], F32R)
        sfc = rt[:, 9, :]
        ps = ctx.enter_context(nc.psum_tensor("ps", [P, 8, HALF], F32))

        def pair(k):
            return ps[:, 2 * k:2 * k + 2, :].rearrange("p a b -> p (a b)")

        cw_scratch = nc.dram_tensor("cw_scratch", [E * GPE, TOK], F32, kind="Internal").ap()
        cw_experts = nc.dram_tensor("cw_experts", [TPH, E, NH * P], F32, kind="Internal").ap()
        b_scratch = nc.dram_tensor("b_scratch", [NS, TOK], F32, kind="Internal").ap()

        s_x = [sem(f"x_loaded{g}") for g in range(NH)]
        s_par = sem("params_loaded")
        s_id = sem("ident_loaded")
        s_win = [sem(f"w_in_loaded{g}") for g in range(2)]
        s_wout = sem("w_out_loaded")
        s_sel = sem("selectors_loaded")
        s_cws = sem("cw_of_experts_stored")
        s_cwg = sem("cw_of_groups_stored")
        s_cwl = [sem(f"cw_rows_loaded{k}") for k in range(RING)]
        s_bw = sem("b_rows_stored")
        s_bbc = sem("b_broadcast")
        s_out = sem("out_stored")

        dve_step = sem("dve_step")
        s_var = sem("variance_ready")
        s_sd = sem("deviation_ready")
        s_x1 = sem("x1_ready")
        s_xn = sem("xn_ready")
        s_tp = sem("transposed")
        s_xnh = sem("xn_high_ready")
        s_xnl = sem("xn_low_ready")
        s_winh = sem("w_in_high_ready")
        s_winl = sem("w_in_low_ready")
        s_inp = sem("in_proj_done")
        s_tap = sem("first_tap_ready")
        s_conv = sem("conv_ready")
        s_xc = sem("xc_ready")
        s_z = sem("silu_z_ready")
        s_xp = [sem(f"x_proj_done{h}") for h in range(NH)]
        s_xs = [sem(f"xs_ready{h}") for h in range(NH)]
        s_dtb = sem("dt_row_broadcast")
        s_xdt = sem("xdt_ready")
        s_c3 = sem("c_parts_ready")
        s_a = sem("a_ready")
        s_ea = sem("exp_a_log_ready")
        s_zero = sem("first_columns_zeroed")
        act_sp = sem("softplus_step")
        s_cor = sem("softplus_correction_ready")
        s_warm = sem("decay_banks_free")
        s_dt = sem("dt_ready")
        s_dtu = sem("dtu_ready")
        s_dd = sem("d_diagonal_ready")
        s_da = sem("decay_ready")
        s_dbu0 = sem("first_dbu_ready")
        s_dbu = sem("dbu_ready")
        s_scan = sem("scan_done")
        s_cb = sem("c_broadcast_done")
        s_hc = sem("hc_ready")
        s_y = sem("y_added")
        s_yz = sem("yz_ready")
        s_o = sem("out_proj_done")
        s_r = sem("last_residual_sum_ready")
        s_sd2 = sem("deviation2_ready")
        s_sd3 = sem("deviation3_ready")
        s_var2 = sem("variance2_ready")
        s_var3 = sem("variance3_ready")
        s_xf = sem("xf_ready")
        s_tp2 = sem("xf_transposed")
        s_lg = sem("logits_done")
        s_sc = sem("scores_ready")
        s_cmb = sem("combine_ready")
        s_cT = sem("combine_transposed")
        s_rwh = sem("router_weights_high_ready")
        s_rwl = sem("router_weights_low_ready")
        s_scT = sem("scores_transposed")
        s_xh = sem("xf_high_ready")
        s_xl = sem("xf_low_ready")
        s_cwT = sem("combine_copied")
        s_g = sem("gate_done")
        s_u = sem("up_done")
        s_d = sem("down_done")
        s_sg = sem("silu_gate_ready")
        s_m1 = sem("gated_ready")
        s_h = sem("h_ready")
        s_hh = sem("h_high_ready")
        s_hl = sem("h_low_ready")
        s_wld = [sem(f"expert_weights_loaded{k}") for k in range(RING)]
        s_wh = sem("w_high_ready")
        s_wl = sem("w_low_ready")
        s_acc = sem("sums_copied")
        s_tp3 = sem("sums_transposed")
        s_var4 = sem("variance4_ready")
        s_sd4 = sem("deviation4_ready")
        s_inv4 = sem("inverse4_ready")
        s_n4 = sem("first_half_normed")
        s_n5 = sem("last_tiles_normed")
        s_fin0 = sem("first_half_ready")
        s_fin = sem("second_half_ready")

        block = ctx.enter_context(nc.Block())

        @block.sync
        def _(sp):
            xt = x.rearrange("b s d -> (b s) d").rearrange("(t p) d -> p t d", p=P)

            def load_x(g):
                sp.dma_start(x_sb[:, g * TPH:(g + 1) * TPH, :], xt[:, g * TPH:(g + 1) * TPH, :]).then_inc(s_x[g], 16)

            def load_w_in(g):
                sp.dma_start(win[:, :, g * DI:(g + 1) * DI], w_in[:, :, g * DI:(g + 1) * DI]).then_inc(s_win[g], 16)

            load_x(0)
            sp.dma_start(idn[:], ident_d).then_inc(s_id, 16)
            sp.dma_start(par[:], params).then_inc(s_par, 16)
            load_x(1)
            load_w_in(0)
            load_w_in(1)
            sp.dma_start(selrow[:], sel_row_d).then_inc(s_sel, 16)
            sp.dma_start(selc[:], sel_c_d).then_inc(s_sel, 16)
            sp.dma_start(wout[:], w_out).then_inc(s_wout, 16)
            sp.dma_start(eb[:], e_bias.rearrange("(a e) -> a e", a=1).to_broadcast([P, E])).then_inc(s_wout, 16)
            for h in range(NH):
                sp.wait_ge(s_xs[h], 1)
            sp.dma_start(b_scratch, xs[0:NS, :]).then_inc(s_bw, 16)
            sp.wait_ge(s_bw, 16)
            sp.wait_ge(s_winl, 2)
            for k in range(4):
                if k:
                    sp.wait_ge(s_bbc, 16 * k)
                if k == 2:
                    sp.wait_ge(s_inp, 2 * NQ)
                src = b_scratch[4 * k:4 * k + 4, :].rearrange("(a n) t -> a n t", a=1).to_broadcast([P, 4, TOK])
                sp.dma_start(bbc[:, 4 * k:4 * k + 4, :], src).then_inc(s_bbc, 16)
            sp.wait_ge(s_dbu, NS * NQ - 1)
            for b in range(RING):
                sp.dma_start(wraw[:, b, :], w_moe[b]).then_inc(s_wld[b], 16)

            def load_weights(slot, b):
                sp.wait_ge(s_wl, b + (1 - RING))
                src = w_moe[bass.ds(b, 1), :, :].rearrange("p a w -> p (a w)") if in_loop(b) else w_moe[b]
                sp.dma_start(wraw[:, slot, :], src).then_inc(s_wld[slot], 16)

            def load_cw(slot, b):
                groups = bass.ds(GPB * b + -GPB * NBS, GPB) if in_loop(b) else slice(GPB * (b - NBS), GPB * (b - NBS + 1))
                src = cw_scratch[groups, :].rearrange("g (a t) -> g a t", a=1).to_broadcast([GPB, GROUP, TOK])
                sp.dma_start(cwrow[:, slot, :], src).then_inc(s_cwl[slot], 16)

            for b in range(NBS, NBS + RING):
                load_weights(b % RING, b)
            sp.wait_ge(s_cwT, 1)
            sp.dma_start(cw_experts.rearrange("t e c -> (t e) c"), cwT[:].rearrange("p h c -> p (h c)")).then_inc(s_cws, 16)
            sp.wait_ge(s_cws, 16)
            for b in range(NBS, NBS + RING):
                for e, lo, hi in experts_of(b - NBS):
                    src = cw_experts[:, e, :].rearrange("t (a c) -> a t c", a=1).to_broadcast([hi - lo, TPH, NH * P])
                    sp.dma_start(cwrow[lo:hi, b % RING, :], src).then_inc(s_cwl[b % RING], 16)
            cw_out = cw_scratch.rearrange("(e k) (t c) -> t e k c", k=GPE, t=TPH)
            for t in range(TPH):
                src = cwT[t * E:(t + 1) * E, :, :].rearrange("e (a h) p -> e a (h p)", a=1).to_broadcast([E, GPE, NH * P])
                sp.dma_start(cw_out[t], src).then_inc(s_cwg, 16)
            sp.wait_ge(s_cwg, 16 * TPH)
            with sp.Fori(2, NB // RING) as m:
                for s in range(RING):
                    load_weights(s, RING * m + s)
                    sp.wait_ge(s_h, 2 * RING * m + 2 * (s + 1 - RING))
                    load_cw(s, RING * m + s)
            for b in range(NB - TAIL, NB):
                load_weights(b % RING, b)
                sp.wait_ge(s_h, 2 * (b + 1 - RING))
                load_cw(b % RING, b)
            ot = out.rearrange("b s d -> (b s) d").rearrange("(t p) d -> p t d", p=P)
            sp.wait_ge(s_fin0, TPH)
            sp.dma_start(ot[:, 0:TPH, :], xn2[:, 0:TPH, :]).then_inc(s_out, 16)
            for t in range(TPH, NT, 2):
                sp.wait_ge(s_fin, t + 2 - TPH)
                sp.dma_start(ot[:, t:t + 2, :], xn2[:, t:t + 2, :]).then_inc(s_out, 16)
            sp.wait_ge(s_out, 16 * (1 + TPH // 2))

        @block.tensor
        def _(pe):
            def keep_warm(n, bank, moving, cols):
                for _ in range(n):
                    mm = nc.tensor.matmul(ps[:, bank, 0:cols], idn[:], moving, start=True, stop=True)
                return mm

            pe.wait_ge(s_id, 16)
            keep_warm(WARM_START, 7, idn[:], P)
            for g in range(NH):
                if g:
                    keep_warm(WARM_BETWEEN, 7, idn[:], P)
                for t in range(g * TPH, (g + 1) * TPH):
                    pe.wait_ge(s_xn, t + 1)
                    for k in range(KD):
                        mm = nc.tensor.transpose(ps[:, 2 * g + k, (t % TPH) * P:(t % TPH + 1) * P],
                                                 xn[:, t, k * P:(k + 1) * P], idn[:])
                mm.then_inc(s_tp, 1)
            keep_warm(WARM_IN_PROJ, 7, idn[:], P)

            def in_proj(j):
                slot = IN_SLOT[j]
                rows = slice(j * P, (j + 1) * P)
                for h in range(NH):
                    if j == 0:
                        pe.wait_ge(s_xnl, KD * (h + 1))
                    cols = slice(h * HALF, (h + 1) * HALF)
                    for k in range(KD):
                        for n, (w, r) in enumerate(((winh, xnh), (winh, xnl), (winl, xnh))):
                            mm = nc.tensor.matmul(ps[:, 2 * slot + h, :], w[:, k, rows], r[:, k, cols],
                                                  start=(k == 0 and n == 0), stop=(k == KD - 1 and n == 2))
                mm.then_inc(s_inp, 1)

            def x_proj(j):
                pe.wait_ge(s_xc, j + 1)
                for h in range(NH):
                    mm = nc.tensor.matmul(ps[0:NX, 2 + h, :], par[:, OFF_XP + j * NX:OFF_XP + (j + 1) * NX],
                                          xc[:, j, h * HALF:(h + 1) * HALF], start=(j == 0), stop=(j == NQ - 1))
                    if j == NQ - 1:
                        mm.then_inc(s_xp[h], 1)

            pe.wait_ge(s_winl, 1)
            pe.wait_ge(s_par, 16)
            for j in range(NQ - 1):
                in_proj(j)
            pe.wait_ge(s_winl, 2)
            in_proj(NQ)
            pe.wait_ge(s_conv, 1)
            in_proj(3)
            pe.wait_ge(s_z, 1)
            x_proj(0)
            x_proj(1)
            pe.wait_ge(s_conv, 3)
            in_proj(NQ + 1)
            x_proj(2)
            x_proj(3)
            pe.wait_ge(s_sel, 32)
            for h in range(NH):
                pe.wait_ge(s_xs[h], 1)
                mm = nc.tensor.matmul(ps[:, 2 + h, :], selrow[:], xs[:, h * HALF:(h + 1) * HALF], start=True, stop=True)
            mm.then_inc(s_dtb, 1)
            in_proj(NQ + 2)
            pe.wait_ge(s_conv, NQ)
            in_proj(NQ + 3)

            def c_bcast(n, wait):
                pe.wait_ge(*wait)
                for h in range(NH):
                    lhs = selc[:, n, :] if not in_loop(n) else selc[:, bass.ds(n, 1), :].rearrange("p a b -> p (a b)")
                    mm = nc.tensor.matmul(ps[:, 4 + h, :], lhs, c3[:, h * HALF:(h + 1) * HALF], start=True, stop=True)
                mm.then_inc(s_cb, 1)

            def y_skip(q, piece):
                cols = bass.ds(piece * QUARTER, QUARTER) if in_loop(piece) else slice(piece * QUARTER, (piece + 1) * QUARTER)
                nc.tensor.matmul(pair(3)[:, cols], ddiag[:, q, :], xc[:, q, cols], start=False, stop=False,
                                 skip_group_check=True)

            def y_add(slot, wait, first=False, last=False):
                pe.wait_ge(*wait)
                for h in range(NH):
                    mm = nc.tensor.matmul(ps[:, 6 + h, :], idn[:], hs[:, slot, h * HALF:(h + 1) * HALF],
                                          start=first, stop=last, skip_group_check=True)
                mm.then_inc(s_y, 1)

            keep_warm(WARM_SOFTPLUS, 0, xc[:, 0, 0:HALF], HALF).then_inc(s_warm, 1)
            pe.wait_ge(s_z, NQ)
            for q in range(NQ):
                for k in range(4):
                    u = NS * q + k
                    c_bcast(k, (s_hc, u) if u else (s_c3, 1))
                    if u == 0:
                        keep_warm(WARM_SCAN, 7, xc[:, 0, 0:HALF], HALF)
                    if k == 1 and q:
                        pe.wait_ge(s_yz, q)
                    if u:
                        y_add((k - 1) % 4, (s_hc, u), first=(k == 1), last=(k == 0))
                    if u == 1:
                        pe.wait_ge(s_dd, 1)
                    if k == 3:
                        y_skip(q, 0)
                with pe.Fori(1, 4) as j:
                    for k in range(4):
                        c_bcast(4 * j + k, (s_hc, 4 * j + (NS * q + k)))
                        y_add((k - 1) % 4, (s_hc, 4 * j + (NS * q + k)))
                        if k == 2:
                            y_skip(q, j)

            def out_proj(t, blocks):
                for q in blocks:
                    mm = nc.tensor.matmul(ps[:, t, 0:D], sz[:, q, t * P:(t + 1) * P], wout[:, q, :],
                                          start=(q == 0), stop=(q == NQ - 1))
                return mm

            def y_add_half(h):
                pe.wait_ge(s_hc, NS * NQ + h)
                nc.tensor.matmul(ps[:, 6 + h, :], idn[:], hs[:, 3, h * HALF:(h + 1) * HALF], start=False, stop=True,
                                 skip_group_check=True).then_inc(s_y, 1)

            pe.wait_ge(s_wout, 32)
            y_add_half(0)
            pe.wait_ge(s_scan, NS * NQ)
            out_proj(0, range(NQ - 1))
            pe.wait_ge(s_yz, NQ)
            out_proj(0, [NQ - 1]).then_inc(s_o, 1)
            for t in range(1, TPH):
                out_proj(t, range(NQ)).then_inc(s_o, 1)
            y_add_half(1)
            out_proj(TPH, range(NQ - 1))
            pe.wait_ge(s_yz, NQ + 1)
            out_proj(TPH, [NQ - 1]).then_inc(s_o, 1)
            for t in range(TPH + 1, NT):
                out_proj(t, range(NQ)).then_inc(s_o, 1)

            def transpose_xf(g):
                for t in range(g * TPH, (g + 1) * TPH):
                    pe.wait_ge(s_xf, t + 1)
                    for k in range(KD):
                        mm = nc.tensor.transpose(ps[:, 2 * k + g, (t % TPH) * P:(t % TPH + 1) * P],
                                                 xn2[:, t, k * P:(k + 1) * P], idn[:])
                mm.then_inc(s_tp2, 1)

            def from_parts(dst, high, low, cols, x_wait=None):
                parts = [(w, xfh, k) for k in range(KD) for w in (high, low)] + [(high, xfl, k) for k in range(KD)]
                for n, (w, r, k) in enumerate(parts):
                    if x_wait is not None and r is xfh and w is high:
                        pe.wait_ge(s_xh, x_wait + k + 1)
                    if x_wait is not None and r is xfl:
                        pe.wait_ge(s_xl, x_wait + k + 1)
                    mm = nc.tensor.matmul(dst, w[k], r[:, k, cols], start=(n == 0), stop=(n == len(parts) - 1),
                                          skip_group_check=True)
                return mm

            def logits(h):
                pe.wait_ge(s_xl, KD * (h + 1))
                pe.wait_ge(s_rwl, 1)
                from_parts(ps[0:E, LOGIT_BANK[h], :], [rwh[:, k, :] for k in range(KD)], [rwl[:, k, :] for k in range(KD)],
                           slice(h * HALF, (h + 1) * HALF)).then_inc(s_lg, 1)

            def transpose_scores():
                pe.wait_ge(s_sc, NH)
                for t in range(NT):
                    mm = nc.tensor.transpose(ps[:, ROUTER_BANK, t * E:(t + 1) * E], scoresT[:, t * P:(t + 1) * P],
                                             idn[0:E, 0:E])
                mm.then_inc(s_scT, 1)

            def transpose_combine():
                pe.wait_ge(s_cmb, 1)
                for h in range(NH):
                    mm = nc.tensor.transpose(ps[:, ROUTER_BANK, h * P:(h + 1) * P], rt[:, 0, h * P:(h + 1) * P], idn[:])
                mm.then_inc(s_cT, 1)

            def three(dst, w_cols, rhs_h, rhs_l, slot, start, stop):
                for n, (w, r) in enumerate(((wh, rhs_h), (wh, rhs_l), (wl, rhs_h))):
                    mm = nc.tensor.matmul(dst, w[:, slot, w_cols], r, start=(start and n == 0), stop=(stop and n == 2),
                                          skip_group_check=True)
                return mm

            def gate_up(half, par2, slot, b, step, up_bank, up_wait, first=False, x_wait=None, between=None):
                cols = slice(half * HALF, (half + 1) * HALF)
                pe.wait_ge(s_wl, b + 1)
                if not first:
                    pe.wait_ge(s_sg, step - 1)

                def weights(w, which):
                    return [w[:, slot, (which * KD + k) * P:(which * KD + k + 1) * P] for k in range(KD)]

                from_parts(ps[:, GATE_BANK[par2], :], weights(wh, 0), weights(wl, 0), cols, x_wait).then_inc(s_g, 1)
                if between is not None:
                    between()
                if up_wait is not None:
                    pe.wait_ge(*up_wait)
                from_parts(ps[:, up_bank, :], weights(wh, 1), weights(wl, 1), cols).then_inc(s_u, 1)

            def routed_gate_up(half, slot, b, step):
                gate_up(half, half, slot, b, step, UP_BANK[half], (s_h, step - 1))

            def down(half, par2, slot, steps, first, last):
                pe.wait_ge(s_hl, steps)
                for dblk in range(KD):
                    mm = three(ps[:, 2 * dblk + half, :], slice(2 * KD * P + dblk * P, 2 * KD * P + (dblk + 1) * P),
                               hh[:, par2, :], hl[:, par2, :], slot, first, last)
                mm.then_inc(s_d, 1)

            def shared_down(i):
                down(i // NBS, i % 2, i % NBS, i + 1, i % NBS == 0, False)

            transpose_xf(0)
            keep_warm(WARM_BETWEEN, 1, idn[:], P)
            pe.wait_ge(s_r, 1)
            for i in range(LEAD):
                if i == NBS:
                    logits(1)
                    transpose_scores()
                    shared_down(i - 1)
                gate_up(i // NBS, i % 2, i % NBS, i % NBS, i, UP_BANK[0], (s_h, i) if i else None, i < 2,
                        None if i else 0, transpose_combine if i == LEAD - 1 else None)
                if i == 0:
                    logits(0)
                if i == NBS - 1:
                    transpose_xf(1)
                if i and i != NBS:
                    shared_down(i - 1)
            gate_up(0, 0, 0, NBS, LEAD, UP_BANK[0], (s_h, LEAD))
            pe.wait_ge(s_cwT, 1)
            with pe.Fori(1, NB // RING) as m:
                for i in range(2 * RING):
                    prev, nxt = (i - 1) % (2 * RING), i + 1
                    down(prev % 2, prev % 2, prev // 2, 2 * RING * m + i, False, False)
                    routed_gate_up(nxt % 2, nxt // 2 % RING, RING * m + nxt // 2, 2 * RING * m + nxt)

            def transpose_sums(h):
                for k in range(KD):
                    pe.wait_ge(s_acc, KD if h == 0 else KD + k + 1)
                    for t in range(h * TPH, (h + 1) * TPH):
                        bank, col = SUM_PLACE[t]
                        mm = nc.tensor.transpose(ps[:, bank, col + k * P:col + (k + 1) * P],
                                                 xc[:, k, t * P:(t + 1) * P], idn[:])
                        if k == KD - 1:
                            mm.then_inc(s_tp3, 1)

            first_step = 2 * (NB - TAIL)
            down(1, 1, (NB - TAIL - 1) % RING, first_step, False, False)
            for i in range(1, 2 * TAIL):
                b = NB - TAIL + i % TAIL
                gate_up(i // TAIL, i % 2, b % RING, b, first_step + i, UP_BANK[i % 2], (s_h, first_step + i - 1))
                down((i - 1) // TAIL, (i - 1) % 2, (NB - TAIL + (i - 1) % TAIL) % RING, first_step + i, False,
                     (i - 1) % TAIL == TAIL - 1)
            transpose_sums(0)
            down(1, 1, (NB - 1) % RING, 2 * NB, False, True)
            transpose_sums(1)

        @block.scalar
        def _(act):
            def deviations_x(g):
                ts = slice(g * TPH, (g + 1) * TPH)
                act.wait_ge(s_var, g + 1)
                nc.scalar.activation(sdv[:, ts, :], dv[:, ts, :], ACT.Sqrt).then_inc(s_sd, 1)

            def w_in_high(g):
                act.wait_ge(s_win[g], 16)
                nc.scalar.copy(winh[:, :, g * DI:(g + 1) * DI], win[:, :, g * DI:(g + 1) * DI]).then_inc(s_winh, 1)

            def xn_high(g):
                act.wait_ge(s_tp, g + 1)
                for k in range(KD):
                    nc.scalar.activation(xnh[:, k, g * HALF:(g + 1) * HALF], ps[:, 2 * g + k, :], ACT.Copy,
                                         scale=par[:, OFF_NW + k:OFF_NW + k + 1]).then_inc(s_xnh, 1)

            deviations_x(0)
            w_in_high(0)
            act.wait_ge(s_par, 16)
            xn_high(0)
            deviations_x(1)
            xn_high(1)
            w_in_high(1)

            def first_tap(j):
                slot = IN_SLOT[j]
                act.wait_ge(s_inp, IN_ORDER.index(j) + 1)
                if j >= 2:
                    act.wait_ge(s_xc, j - 1)
                nc.scalar.activation(cacc[:, j % 2, :], pair(slot), ACT.Identity,
                                     scale=par[:, OFF_CONV + j * KC + KC - 1:OFF_CONV + j * KC + KC],
                                     bias=par[:, OFF_CB + j:OFF_CB + j + 1]).then_inc(s_tap, 1)

            def silu_xc(j):
                act.wait_ge(s_conv, j + 1)
                nc.scalar.activation(xc[:, j, :], cacc[:, j % 2, :], ACT.Silu).then_inc(s_xc, 1)

            def silu_z(j):
                act.wait_ge(s_inp, IN_ORDER.index(NQ + j) + 1)
                nc.scalar.activation(sz[:, j, :], pair(IN_SLOT[NQ + j]), ACT.Silu).then_inc(s_z, 1)

            def softplus(q, steps=range(5)):
                sc, bi = par[:, OFF_DTW + q:OFF_DTW + q + 1], par[:, OFF_DTB + q:OFF_DTB + q + 1]
                n = 5 * q
                row = xdt[:] if q else pair(1)
                if 0 in steps:
                    if q:
                        act.wait_ge(s_dt, q)
                    nc.scalar.activation(sp_abs[:], row, ACT.Abs, scale=sc, bias=bi).then_inc(act_sp, 1)
                if 1 in steps:
                    act.wait_ge(act_sp, n + 1)
                    nc.scalar.activation(sp_exp[:], sp_abs[:], ACT.Exp, scale=-1.0).then_inc(act_sp, 1)
                if 2 in steps:
                    act.wait_ge(act_sp, n + 2)
                    nc.scalar.activation(sp_w[:], sp_exp[:], ACT.Identity, bias=1.0).then_inc(act_sp, 1)
                if 3 in steps:
                    nc.scalar.activation(sp_relu[:], row, ACT.Relu, scale=sc, bias=bi).then_inc(act_sp, 1)
                if 4 in steps:
                    act.wait_ge(act_sp, n + 3)
                    nc.scalar.activation(sp_abs[:], sp_w[:], ACT.Ln).then_inc(act_sp, 1)

            first_tap(0)
            first_tap(1)
            silu_xc(0)
            first_tap(2)
            silu_z(0)
            silu_xc(1)
            first_tap(3)
            silu_xc(2)
            silu_xc(3)
            silu_z(1)
            act.wait_ge(s_xp[0], 1)
            nc.scalar.copy(xs[:, 0:HALF], ps[0:NX, 2, :]).then_inc(s_xs[0], 1)
            nc.scalar.preload_act_table_set("natural_log_exp_and_others")
            nc.scalar.activation(a_sb[:], par[:, OFF_AL:OFF_AL + NQ * NS], ACT.Exp).then_inc(s_ea, 1)
            act.wait_ge(s_dtb, 1)
            softplus(0)
            nc.scalar.copy(xdt[:], pair(1)).then_inc(s_xdt, 1)
            silu_z(2)
            silu_z(3)
            nc.scalar.preload_act_table_set("natural_log_exp_and_others")

            def decay(q, n, slot, wait):
                act.wait_ge(*wait)
                dst = pair(slot).rearrange("p (b s) -> p b s", b=BATCH)[:, :, 1:SEQ]
                src = dt[:, q % 2, :].rearrange("p (b s) -> p b s", b=BATCH)[:, :, 1:SEQ]
                sc = a_sb[:, bass.ds(n + NS * q, 1)] if in_loop(n) else a_sb[:, NS * q + n:NS * q + n + 1]
                nc.scalar.activation(dst, src, ACT.Exp, scale=sc).then_inc(s_da, 1)

            act.wait_ge(s_zero, 1)
            act.wait_ge(s_a, 1)
            act.wait_ge(s_xdt, 1)
            for q in range(NQ):
                act.wait_ge(s_dt, q + 1)
                for k in range(4):
                    u = NS * q + k
                    decay(q, k, k % 2, (s_scan, u - 1) if u >= 2 else (s_zero, 1))
                    if k and q + 1 < NQ:
                        softplus(q + 1, ((), (0,), (1, 2), (3, 4))[k])
                with act.Fori(1, 4) as j:
                    for k in range(4):
                        decay(q, 4 * j + k, k % 2, (s_scan, 4 * j + (NS * q + k - 1)))

            def w_high(slot, wait_load, wait_down):
                act.wait_ge(s_wld[slot], wait_load)
                if wait_down is not None:
                    act.wait_ge(s_d, wait_down)
                nc.scalar.copy(wh[:, slot, :], wraw[:, slot, :]).then_inc(s_wh, 1)

            def deviation(g, s_v, s_dev):
                ts = slice(g * TPH, (g + 1) * TPH)
                act.wait_ge(s_v, g + 1)
                nc.scalar.activation(sd[:, ts], mv[:, ts, 1], ACT.Sqrt).then_inc(s_dev, 1)

            def x_high(g):
                act.wait_ge(s_tp2, g + 1)
                for k in range(KD):
                    nc.scalar.copy(xfh[:, k, g * HALF:(g + 1) * HALF], ps[:, 2 * k + g, :]).then_inc(s_xh, 1)

            def silu_gate(par2, step, first=False):
                act.wait_ge(s_g, step + 1)
                if not first:
                    act.wait_ge(s_h, step - 1)
                nc.scalar.activation(sg[:, par2, :], ps[:, GATE_BANK[par2], :], ACT.Silu).then_inc(s_sg, 1)

            def h_high(par2, step, first=False):
                act.wait_ge(s_h, step + 1)
                if not first:
                    act.wait_ge(s_d, step - 1)
                nc.scalar.copy(hh[:, par2, :], hbuf[:, par2, :]).then_inc(s_hh, 1)

            for b in range(NBS):
                w_high(b, 16, None)
            nc.scalar.copy(rwh[:], par[:, OFF_RW:OFF_RW + KD * E].rearrange("p (k e) -> p k e", k=KD)).then_inc(s_rwh, 1)
            deviation(0, s_var2, s_sd2)
            deviation(0, s_var3, s_sd3)
            x_high(0)
            deviation(1, s_var2, s_sd2)
            for i in range(LEAD):
                silu_gate(i % 2, i, i < 2)
                if i == 1:
                    deviation(1, s_var3, s_sd3)
                if i == LEAD - 1:
                    act.wait_ge(s_cT, 1)
                    nc.scalar.copy(cwT[:], ps[:, ROUTER_BANK, 0:NH * P].rearrange("p (h t) -> p h t", h=NH)).then_inc(s_cwT, 1)
                    w_high(0, 32, NBS + 1)
                if i == NBS - 1:
                    x_high(1)
                h_high(i % 2, i, i < 2)
                if i == NBS - 1:
                    for h in range(NH):
                        act.wait_ge(s_lg, h + 1)
                        nc.scalar.activation(scoresT[:, h * HALF:(h + 1) * HALF], ps[0:E, LOGIT_BANK[h], :],
                                             ACT.Sigmoid).then_inc(s_sc, 1)
            with act.Fori(1, NB // RING) as m:
                for s in range(RING):
                    silu_gate(0, 2 * RING * m + 2 * s)
                    h_high(0, 2 * RING * m + 2 * s)
                    if s + 1 < RING:
                        w_high(s + 1, 16 * m + 16, 2 * RING * m + (2 * (s + 1) - 3))
                    else:
                        w_high(0, 16 * m + 32, 2 * RING * m + (2 * RING - 3))
                    silu_gate(1, 2 * RING * m + (2 * s + 1))
                    h_high(1, 2 * RING * m + (2 * s + 1))
            w_high((NB - 1) % RING, 16 * ((NB - 1) // RING + 1), 2 * (NB - 1) - 3)
            for i in range(2 * TAIL):
                silu_gate(i % 2, 2 * (NB - TAIL) + i)
                h_high(i % 2, 2 * (NB - TAIL) + i)
                if i == TAIL:
                    act.wait_ge(s_d, 2 * NB - TAIL)
                    for k in range(KD):
                        nc.scalar.copy(xc[:, k, 0:HALF], ps[:, 2 * k, :]).then_inc(s_acc, 1)
            deviation(0, s_var4, s_sd4)
            act.wait_ge(s_d, 2 * NB)
            for k in range(KD):
                nc.scalar.copy(xc[:, k, HALF:TOK], ps[:, 2 * k + 1, :]).then_inc(s_acc, 1)
            deviation(1, s_var4, s_sd4)
            act.wait_ge(s_inv4, 1)
            for t in range(NT - 2, NT):
                bank, col = SUM_PLACE[t]
                nc.scalar.activation(x1[:, t, :], ps[:, bank, col:col + D], ACT.Identity, scale=rstd[:, t:t + 1],
                                     bias=nmr[:, t:t + 1]).then_inc(s_n5, 1)

        @block.gpsimd
        def _(pool):
            for g in range(2):
                rows = slice(g * DI, (g + 1) * DI)
                pool.wait_ge(s_winh, g + 1)
                nc.gpsimd.tensor_tensor(winl[:, :, rows], win[:, :, rows], winh[:, :, rows].bitcast(F32),
                                        ALU.subtract).then_inc(s_winl, 1)
            for t in range(NT):
                pool.wait_ge(s_xn, t + 1)
                nc.gpsimd.tensor_scalar(x1[:, t, :], x_sb[:, t, :], mv[:, t, 0:1], rdv[:, t, 0:1], ALU.subtract,
                                        ALU.mult).then_inc(s_x1, 1)

            def make_dtu(q):
                pool.wait_ge(s_dt, q + 1)
                if q >= 2:
                    pool.wait_ge(s_dbu, NS * (q - 1) - 1)
                nc.gpsimd.tensor_tensor(dtu[:, q % 2, :], dt[:, q % 2, :], xc[:, q, :], ALU.mult).then_inc(s_dtu, 1)

            def dbu_unit(q, n, slot, wait):
                if wait is not None:
                    pool.wait_ge(*wait)
                src = bbc[:, bass.ds(n, 1), :].rearrange("p a b -> p (a b)") if in_loop(n) else bbc[:, n, :]
                nc.gpsimd.tensor_tensor(dbu[:, slot, :], dtu[:, q % 2, :], src, ALU.mult).then_inc(s_dbu, 1)

            for q in range(NQ):
                pool.wait_ge(s_dtu, q + 1)
                if q == 0:
                    pool.wait_ge(s_bbc, 16)
                for k in range(q == 0, 4):
                    u = NS * q + k
                    dbu_unit(q, k, k, (s_scan, u - 3) if u >= 4 else None)
                with pool.Fori(1, 4) as j:
                    if q == 0:
                        pool.wait_ge(s_bbc, 16 * j + 16)
                    for k in range(4):
                        dbu_unit(q, 4 * j + k, k, (s_scan, 4 * j + (NS * q + k - 3)))
                if q + 1 < NQ:
                    make_dtu(q + 1)

            def w_low_pool(slot, b):
                pool.wait_ge(s_wh, b + 1)
                nc.gpsimd.tensor_tensor(wl[:, slot, :], wraw[:, slot, :], wh[:, slot, :].bitcast(F32),
                                        ALU.subtract).then_inc(s_wl, 1)

            for b in range(NBS):
                w_low_pool(b, b)
            pool.wait_ge(s_rwh, 1)
            nc.gpsimd.tensor_tensor(rwl[:], par[:, OFF_RW:OFF_RW + KD * E].rearrange("p (k e) -> p k e", k=KD),
                                    rwh[:].bitcast(F32), ALU.subtract).then_inc(s_rwl, 1)

            def low(par2, step, first):
                pool.wait_ge(s_hh, step + 1)
                if not first:
                    pool.wait_ge(s_d, step - 1)
                nc.gpsimd.tensor_tensor(hl[:, par2, :], hbuf[:, par2, :], hh[:, par2, :].bitcast(F32),
                                        ALU.subtract).then_inc(s_hl, 1)

            for i in range(LEAD):
                if i == LEAD - 1:
                    w_low_pool(0, NBS)
                low(i % 2, i, i < 2)
            with pool.Fori(1, NB // RING) as m:
                for i in range(2 * RING):
                    low(i % 2, 2 * RING * m + i, False)
            for i in range(2 * (NB - TAIL), 2 * NB):
                low(i % 2, i, False)
            for t in range(TPH):
                pool.wait_ge(s_n4, t + 1)
                nc.gpsimd.tensor_tensor(xn2[:, t, :], x2[:, t, :], x1[:, t, :], ALU.add).then_inc(s_fin0, 1)

        @block.vector
        def _(dve):
            count = [0]

            def after(ins):
                count[0] += 1
                ins.then_inc(dve_step, 1)
                dve.wait_ge(dve_step, count[0])

            def aggregate(g, s_ready):
                for t in range(g * TPH, (g + 1) * TPH):
                    last = nc.vector.bn_aggr(mv[:, t, :], stats[:, t, :])
                after(last)
                ts = slice(g * TPH, (g + 1) * TPH)
                nc.vector.tensor_scalar(mv[:, ts, 1], mv[:, ts, 1], EPS, None, ALU.add).then_inc(s_ready, 1)

            def moments(src, g, s_ready):
                for t in range(g * TPH, (g + 1) * TPH):
                    last = nc.vector.bn_stats(stats[:, t, :], src(t))
                after(last)
                aggregate(g, s_ready)

            def inverse(g, s_dev):
                ts = slice(g * TPH, (g + 1) * TPH)
                dve.wait_ge(s_dev, g + 1)
                after(nc.vector.reciprocal(rstd[:, ts], sd[:, ts]))

            def normed(dst, src, t):
                return nc.vector.tensor_scalar(dst, src, mv[:, t, 0:1], rstd[:, t:t + 1], ALU.subtract, ALU.mult)

            def both_norms(g):
                ts = slice(g * TPH, (g + 1) * TPH)
                dve.wait_ge(s_x[g], 16)
                for t in range(g * TPH, (g + 1) * TPH):
                    last = nc.vector.bn_stats(stats[:, t, :], x_sb[:, t, :])
                after(last)
                for t in range(g * TPH, (g + 1) * TPH):
                    last = nc.vector.bn_aggr(mv[:, t, :], stats[:, t, :])
                after(last)
                after(nc.vector.tensor_scalar(dv[:, ts, 0], mv[:, ts, 1], EPS, None, ALU.add))
                nc.vector.scalar_tensor_tensor(out=dv[:, ts, 1], in0=dv[:, ts, 0], scalar=EPS, in1=mv[:, ts, 1],
                                               op0=ALU.mult, op1=ALU.add).then_inc(s_var, 1)
                dve.wait_ge(s_sd, g + 1)
                after(nc.vector.reciprocal(rdv[:, ts, :], sdv[:, ts, :]))
                for t in range(g * TPH, (g + 1) * TPH):
                    nc.vector.tensor_scalar(xn[:, t, :], x_sb[:, t, :], mv[:, t, 0:1], rdv[:, t, 1:2], ALU.subtract,
                                            ALU.mult).then_inc(s_xn, 1)

            def xn_low(g):
                dve.wait_ge(s_par, 16)
                for k in range(KD):
                    cols, nw = slice(g * HALF, (g + 1) * HALF), par[:, OFF_NW + k:OFF_NW + k + 1]
                    dve.wait_ge(s_xnh, KD * g + k + 1)
                    nc.vector.scalar_tensor_tensor(out=xnl[:, k, cols], in0=ps[:, 2 * g + k, :], scalar=nw,
                                                   in1=xnh[:, k, cols].bitcast(F32), op0=ALU.mult,
                                                   op1=ALU.subtract).then_inc(s_xnl, 1)

            both_norms(0)
            both_norms(1)
            xn_low(0)
            xn_low(1)
            for q in range(NQ):
                last = nc.vector.tensor_scalar(ddiag[:, q, :], idn[:], par[:, OFF_DP + q:OFF_DP + q + 1], None, ALU.mult)
            last.then_inc(s_dd, 1)
            for j in range(NQ):
                slot = IN_SLOT[j]
                xi = pair(slot).rearrange("p (b s) -> p b s", b=BATCH)
                acc = cacc[:, j % 2, :].rearrange("p (b s) -> p b s", b=BATCH)
                dve.wait_ge(s_tap, j + 1)
                for shift in range(1, KC):
                    w = par[:, OFF_CONV + j * KC + KC - 1 - shift:OFF_CONV + j * KC + KC - shift]
                    ins = nc.vector.scalar_tensor_tensor(out=acc[:, :, shift:SEQ], in0=xi[:, :, 0:SEQ - shift], scalar=w,
                                                         in1=acc[:, :, shift:SEQ], op0=ALU.mult, op1=ALU.add)
                    if shift < KC - 1:
                        after(ins)
                    else:
                        ins.then_inc(s_conv, 1)

            dve.wait_ge(s_xp[1], 1)
            nc.vector.tensor_copy(xs[:, HALF:TOK], ps[0:NX, 3, :]).then_inc(s_xs[1], 1)
            for h in range(NH):
                dve.wait_ge(s_xs[h], 1)
            after(nc.vector.tensor_copy(c3[0:2 * NS, :], xs[0:2 * NS, :]))
            after(nc.vector.tensor_tensor(cres[:, 0, :], xs[0:2 * NS, :], c3[0:2 * NS, :], ALU.subtract))
            after(nc.vector.tensor_copy(cmid[:], cres[:, 0, :]))
            after(nc.vector.tensor_tensor(cres[:, 1, :], cres[:, 0, :], cmid[:], ALU.subtract))
            nc.vector.tensor_copy(c3[2 * NS:4 * NS, :], cmid[:])
            nc.vector.tensor_copy(c3[4 * NS:6 * NS, :], cres[:, 1, :]).then_inc(s_c3, 1)
            dve.wait_ge(s_ea, 1)
            nc.vector.tensor_scalar(a_sb[:], a_sb[:], -1.0, None, ALU.mult).then_inc(s_a, 1)

            def correction(q):
                dve.wait_ge(act_sp, 5 * q + 3)
                nc.vector.scalar_tensor_tensor(out=sp_exp[:], in0=sp_w[:], scalar=1.0, in1=sp_exp[:],
                                               op0=ALU.subtract, op1=ALU.subtract).then_inc(s_cor, 1)

            def corrected(q):
                dve.wait_ge(act_sp, 5 * q + 4)
                dve.wait_ge(s_cor, 2 * q + 1)
                nc.vector.tensor_tensor(sp_relu[:], sp_relu[:], sp_exp[:], ALU.subtract).then_inc(s_cor, 1)

            def make_dt(q):
                dve.wait_ge(act_sp, 5 * q + 5)
                dve.wait_ge(s_cor, 2 * q + 2)
                if q >= 2:
                    dve.wait_ge(s_da, NS * (q - 1))
                    dve.wait_ge(s_dtu, q - 1)
                nc.vector.tensor_tensor(dt[:, q % 2, :], sp_relu[:], sp_abs[:], ALU.add).then_inc(s_dt, 1)

            def scan(slot2, slot4, u, wait_y):
                dve.wait_ge(s_da, u + 1)
                first = not wait_y and u == 0
                dve.wait_ge(s_dbu0 if first else s_dbu, 1 if first else u)
                if wait_y:
                    dve.wait_ge(s_y, u - 3)
                nc.vector.tensor_tensor_scan(hs[:, slot4, :], pair(slot2), dbu[:, slot4, :], 0.0,
                                             ALU.mult, ALU.add).then_inc(s_scan, 1)

            def times_c(slot4, u1):
                dve.wait_ge(s_scan, u1)
                dve.wait_ge(s_cb, u1)
                nc.vector.tensor_tensor(hs[:, slot4, :], hs[:, slot4, :], pair(2), ALU.mult).then_inc(s_hc, 1)

            def gate_y(q):
                dve.wait_ge(s_y, NS * (q + 1))
                nc.vector.tensor_tensor(sz[:, q, :], pair(3), sz[:, q, :], ALU.mult).then_inc(s_yz, 1)

            correction(0)
            corrected(0)
            make_dt(0)
            dve.wait_ge(s_dt, 1)
            nc.vector.tensor_tensor(dtu[:, 0, :], dt[:, 0, :], xc[:, 0, :], ALU.mult).then_inc(s_dtu, 1)
            dve.wait_ge(s_z, 2)
            dve.wait_ge(s_xdt, 1)
            dve.wait_ge(s_warm, 1)
            nc.vector.memset(ps[:, 0:4, :].rearrange("p a (b s) -> p (a b) s", s=SEQ)[:, :, 0:1], 0.0).then_inc(s_zero, 1)
            dve.wait_ge(s_bbc, 16)
            dve.wait_ge(s_dtu, 1)
            nc.vector.tensor_tensor(dbu[:, 0, :], dtu[:, 0, :], bbc[:, 0, :], ALU.mult).then_inc(s_dbu0, 1)
            dve.wait_ge(s_c3, 1)
            for q in range(NQ):
                for k in range(4):
                    u = NS * q + k
                    scan(k % 2, k, u, u >= 4)
                    if u:
                        times_c((k - 1) % 4, u)
                    if k == 1 and q:
                        gate_y(q - 1)
                for k in range(4):
                    if q + 1 < NQ and k < 3:
                        (correction, corrected, make_dt)[k](q + 1)
                    scan(k % 2, k, NS * q + 4 + k, True)
                    times_c((k - 1) % 4, NS * q + 4 + k)
                with dve.Fori(2, 4) as j:
                    for k in range(4):
                        scan(k % 2, k, 4 * j + (NS * q + k), True)
                        times_c((k - 1) % 4, 4 * j + (NS * q + k))
            for h in range(NH):
                cols = slice(h * HALF, (h + 1) * HALF)
                dve.wait_ge(s_scan, NS * NQ)
                dve.wait_ge(s_cb, NS * NQ)
                nc.vector.tensor_tensor(hs[:, 3, cols], hs[:, 3, cols], ps[:, 4 + h, :], ALU.mult).then_inc(s_hc, 1)

            def gate_last(h):
                cols = slice(h * HALF, (h + 1) * HALF)
                dve.wait_ge(s_y, NS * NQ + h)
                nc.vector.tensor_tensor(sz[:, NQ - 1, cols], ps[:, 6 + h, :], sz[:, NQ - 1, cols],
                                        ALU.mult).then_inc(s_yz, 1)

            gate_last(0)

            def resid(t):
                dve.wait_ge(s_o, t + 1)
                return nc.vector.tensor_tensor(x1[:, t, :], ps[:, t, 0:D], x1[:, t, :], ALU.add)

            def norm_sum(g):
                inverse(g, s_sd2)
                for t in range(g * TPH, (g + 1) * TPH):
                    last = normed(x1[:, t, :], x1[:, t, :], t)
                return last

            def norm_x2(g):
                inverse(g, s_sd3)
                for t in range(g * TPH, (g + 1) * TPH):
                    normed(xn2[:, t, :], x2[:, t, :], t).then_inc(s_xf, 1)

            def make_x2(g):
                for t in range(g * TPH, (g + 1) * TPH):
                    last = nc.vector.tensor_tensor(x2[:, t, :], x_sb[:, t, :], x1[:, t, :], ALU.add)
                return last

            def x_low(g):
                for k in range(KD):
                    cols = slice(g * HALF, (g + 1) * HALF)
                    dve.wait_ge(s_xh, KD * g + k + 1)
                    nc.vector.tensor_tensor(xfl[:, k, cols], ps[:, 2 * k + g, :], xfh[:, k, cols].bitcast(F32),
                                            ALU.subtract).then_inc(s_xl, 1)

            def w_low(slot, wait_high):
                dve.wait_ge(s_wh, wait_high)
                nc.vector.tensor_tensor(wl[:, slot, :], wraw[:, slot, :], wh[:, slot, :].bitcast(F32),
                                        ALU.subtract).then_inc(s_wl, 1)

            def shared_step(par2, step):
                dve.wait_ge(s_sg, step + 1)
                dve.wait_ge(s_u, step + 1)
                if step >= 2:
                    dve.wait_ge(s_hl, step - 1)
                nc.vector.tensor_tensor(hbuf[:, par2, :], ps[:, UP_BANK[0], :], sg[:, par2, :], ALU.mult).then_inc(s_h, 1)

            dve.wait_ge(s_x1, NT)
            for t in range(TPH):
                after(resid(t))
                last = nc.vector.bn_stats(stats[:, t, :], x1[:, t, :])
            after(last)
            aggregate(0, s_var2)
            gate_last(1)
            after(norm_sum(0))
            after(make_x2(0))
            moments(lambda t: x2[:, t, :], 0, s_var3)
            norm_x2(0)
            for t in range(TPH, NT):
                last = resid(t)
            last.then_inc(s_r, 1)
            x_low(0)
            dve.wait_ge(s_r, 1)
            moments(lambda t: x1[:, t, :], 1, s_var2)
            after(norm_sum(1))
            shared_step(0, 0)
            after(make_x2(1))
            moments(lambda t: x2[:, t, :], 1, s_var3)
            shared_step(1, 1)
            norm_x2(1)
            shared_step(0, 2)
            x_low(1)

            def r3(a):
                return a.rearrange("p (t e) -> p t e", t=NT)

            def r4(a):
                return a.rearrange("p (t g e) -> p t g e", t=NT, g=NG)

            scores = ps[:, ROUTER_BANK, 0:NT * E]
            dve.wait_ge(s_wout, 32)
            dve.wait_ge(s_scT, 1)
            ebb = eb[:].rearrange("p (a e) -> p a e", a=1).to_broadcast([P, NT, E])
            after(nc.vector.tensor_tensor(r3(sfc), r3(scores), ebb, ALU.add))
            W = NT * NG

            def v(slot, part):
                return rt[:, slot, part * W:(part + 1) * W].rearrange("p (t g) -> p t g", t=NT)

            def pairs(part):
                return rt[:, 1, 2 * part * W:2 * (part + 1) * W].rearrange("p (t g e) -> p t g e", t=NT, g=NG)

            even, odd = r4(sfc)[:, :, :, 0:GE:2], r4(sfc)[:, :, :, 1:GE:2]
            nc.vector.tensor_tensor(pairs(0), even, odd, ALU.max)
            after(nc.vector.tensor_tensor(pairs(1), even, odd, ALU.min))
            nc.vector.tensor_tensor(v(2, 0), pairs(0)[:, :, :, 0], pairs(0)[:, :, :, 1], ALU.max)
            nc.vector.tensor_tensor(v(2, 1), pairs(0)[:, :, :, 0], pairs(0)[:, :, :, 1], ALU.min)
            after(nc.vector.tensor_tensor(v(2, 2), pairs(1)[:, :, :, 0], pairs(1)[:, :, :, 1], ALU.max))
            after(nc.vector.tensor_tensor(v(2, 3), v(2, 1), v(2, 2), ALU.max))
            after(nc.vector.tensor_tensor(v(3, 0), v(2, 0), v(2, 3), ALU.add))
            for t in range(NT):
                last = nc.vector.max(rt[:, 5, t * NG:(t + 1) * NG], v(3, 0)[:, t, :])
            after(last)
            after(nc.vector.memset(rt[:, 5, 0:NT * NG].rearrange("p (t g) -> p t g", t=NT)[:, :, TKG:NG], NO_SCORE))
            for t in range(NT):
                last = nc.vector.match_replace(out=v(3, 1)[:, t, :], in_to_replace=rt[:, 5, t * NG:(t + 1) * NG],
                                               in_values=v(3, 0)[:, t, :], imm_value=MARK)
            shared_step(1, 3)
            after(last)
            after(nc.vector.tensor_scalar(v(2, 0), v(3, 1), MARK, None, ALU.is_equal))
            gm = rt[:, 2, 0:W].rearrange("p (t g e) -> p t g e", t=NT, e=1).to_broadcast([P, NT, NG, GE])
            after(nc.vector.tensor_tensor(r4(rt[:, 4, :]), r4(sfc), gm, ALU.mult))
            after(nc.vector.tensor_scalar(rt[:, 4, :], rt[:, 4, :], 0.0, None, ALU.add))
            for t in range(NT):
                last = nc.vector.max(rt[:, 5, t * TOPK:(t + 1) * TOPK], rt[:, 4, t * E:(t + 1) * E])
            shared_step(0, 4)
            after(last)
            for t in range(NT):
                last = nc.vector.match_replace(out=rt[:, 6, t * E:(t + 1) * E],
                                               in_to_replace=rt[:, 5, t * TOPK:(t + 1) * TOPK],
                                               in_values=rt[:, 4, t * E:(t + 1) * E], imm_value=MARK)
            after(last)
            after(nc.vector.scalar_tensor_tensor(out=rt[:, 7, :], in0=rt[:, 6, :], scalar=MARK, in1=scores,
                                                 op0=ALU.is_equal, op1=ALU.mult))
            after(nc.vector.tensor_reduce(rt[:, 5, 0:NT], r3(rt[:, 7, :]), AX.X, ALU.add))
            after(nc.vector.tensor_scalar(rt[:, 5, 0:NT], rt[:, 5, 0:NT], 1e-20, None, ALU.add))
            after(nc.vector.reciprocal(rt[:, 5, NT:2 * NT], rt[:, 5, 0:NT]))
            inv = rt[:, 5, NT:2 * NT].rearrange("p (t e) -> p t e", e=1).to_broadcast([P, NT, E])
            nc.vector.scalar_tensor_tensor(out=r3(rt[:, 0, :]), in0=r3(rt[:, 7, :]), scalar=SCALE, in1=inv,
                                           op0=ALU.mult, op1=ALU.mult).then_inc(s_cmb, 1)
            shared_step(1, 5)

            def extra(slot):
                return 16 * (len(experts_of(slot)) - 1)

            def routed_step(half, par2, slot, step, loads):
                dve.wait_ge(s_sg, step + 1)
                dve.wait_ge(s_cwl[slot], loads)
                dve.wait_ge(s_h, step - 1)
                weights = cwrow[:, slot, :].rearrange("p (t h c) -> p h t c", t=TPH, h=NH)[:, half, :, :]
                nc.vector.tensor_tensor(m1[:, par2, :].rearrange("p (t c) -> p t c", t=TPH), weights,
                                        sg[:, par2, :].rearrange("p (t c) -> p t c", t=TPH), ALU.mult).then_inc(s_m1, 1)
                dve.wait_ge(s_m1, step + (1 - LEAD))
                dve.wait_ge(s_u, step + 1)
                dve.wait_ge(s_hl, step - 1)
                nc.vector.tensor_tensor(hbuf[:, par2, :], ps[:, UP_BANK[par2], :], m1[:, par2, :], ALU.mult).then_inc(s_h, 1)

            with dve.Fori(1, NB // RING) as m:
                for s in range(RING):
                    routed_step(0, 0, s, 2 * RING * m + 2 * s, 16 * m + extra(s))
                    w_low((s + 1) % RING, RING * m + (s + 2))
                    routed_step(1, 1, s, 2 * RING * m + (2 * s + 1), 16 * m + extra(s))
            w_low((NB - 1) % RING, NB)
            for i in range(2 * TAIL):
                b = NB - TAIL + i % TAIL
                routed_step(i // TAIL, i % 2, b % RING, 2 * (NB - TAIL) + i, 16 * (b // RING) + extra(b % RING))

            def sums(t):
                bank, col = SUM_PLACE[t]
                return ps[:, bank, col:col + D]

            def sum_moments(g):
                for t in range(g * TPH, (g + 1) * TPH):
                    dve.wait_ge(s_tp3, max(t + 1, TPH))
                    last = nc.vector.bn_stats(stats[:, t, :], sums(t))
                after(last)
                aggregate(g, s_var4)

            sum_moments(0)
            inverse(0, s_sd4)
            for t in range(TPH):
                normed(x1[:, t, :], sums(t), t).then_inc(s_n4, 1)
            sum_moments(1)
            inverse(1, s_sd4)
            nc.vector.scalar_tensor_tensor(out=nmr[:, TPH:NT], in0=mv[:, TPH:NT, 0], scalar=-1.0, in1=rstd[:, TPH:NT],
                                           op0=ALU.mult, op1=ALU.mult).then_inc(s_inv4, 1)
            for t in range(TPH, NT - 2):
                last = normed(x1[:, t, :], sums(t), t)
            after(last)
            for t in range(TPH, NT):
                if t >= NT - 2:
                    dve.wait_ge(s_n5, t - (NT - 3))
                nc.vector.tensor_tensor(xn2[:, t, :], x2[:, t, :], x1[:, t, :], ALU.add).then_inc(s_fin, 1)


def in_loop(n):
    return not isinstance(n, int)


def kernel(**inputs):
    import concourse.bacc as bacc
    import ml_dtypes
    from concourse.bass_utils import run_bass_kernel_spmd as run

    def a(name):
        return np.asarray(inputs["L0_" + name])

    def rows(m, n):
        return m.reshape(n, P, -1).transpose(1, 0, 2)

    params = np.concatenate([
        rows(a("attn_norm_w"), KD).reshape(P, -1),
        rows(a("attn_conv_w").reshape(DI, KC), NQ).reshape(P, -1),
        rows(a("attn_conv_b"), NQ).reshape(P, -1),
        rows(a("attn_x_proj_w").T, NQ).reshape(P, -1),
        rows(a("attn_dt_w"), NQ).reshape(P, -1),
        rows(a("attn_dt_b"), NQ).reshape(P, -1),
        rows(a("attn_A_log"), NQ).reshape(P, -1),
        rows(a("attn_D_param"), NQ).reshape(P, -1),
        rows(a("ffn_router_weight").T, KD).reshape(P, -1),
    ], axis=1)
    pad = np.zeros((NB * P - E * I - SI, D), np.float32)

    def blocks(routed, shared):
        return np.concatenate([shared, pad, routed]).reshape(NB, P, D)

    def stationary(w):
        return w.reshape(NB, P, KD, P).transpose(0, 3, 2, 1).reshape(NB, P, KD * P)

    gate = stationary(blocks(a("ffn_Wg").reshape(E * I, D), a("ffn_sWg")))
    up = stationary(blocks(a("ffn_Wu").reshape(E * I, D), a("ffn_sWu")))
    down = blocks(a("ffn_Wd").transpose(0, 2, 1).reshape(E * I, D), a("ffn_sWd").T)
    sel_row = np.zeros((NX, P), np.float32)
    sel_row[NX - 1] = 1
    sel_c = np.zeros((3, 2 * NS, NS, P), ml_dtypes.bfloat16)
    for n in range(NS):
        sel_c[:, NS + n, n] = 1
    arrays = {
        "x": a("attn_x"),
        "w_in": rows(a("attn_in_proj_w").T, KD),
        "params": params,
        "w_out": rows(a("attn_out_proj_w").T, NQ),
        "e_bias": a("ffn_e_bias"),
        "w_moe": np.concatenate([gate, up, down], axis=2),
        "ident": np.eye(P, dtype=np.float32),
        "sel_row": sel_row,
        "sel_c": sel_c.reshape(3 * 2 * NS, NS, P),
    }
    arrays = {n: np.ascontiguousarray(v) for n, v in arrays.items()}
    nc = bacc.Bacc("TRN2", target_bir_lowering=False, num_devices=1)
    aps = [nc.dram_tensor(n, v.shape, mybir.dt.from_np(v.dtype), kind="ExternalInput").ap() for n, v in arrays.items()]
    aps.append(nc.dram_tensor("out", (BATCH, SEQ, D), F32, kind="ExternalOutput").ap())
    build(nc, *aps)
    return run(nc, [arrays], core_ids=[0]).results[0]["out"]
```
